# Optimizing a Trainium2 kernel written in Bass

```python
import numpy as np
import jax
import jax.numpy as jnp

def _softmax(x, axis=-1):
    return jax.nn.softmax(x, axis=axis)

def _gelu(x):
    return jax.nn.gelu(x, approximate=True)

def _silu(x):
    return jax.nn.silu(x)

def _sigmoid(x):
    return jax.nn.sigmoid(x)

def _layernorm(x, axis=-1, eps=1e-05):
    m = jnp.mean(x, axis=axis, keepdims=True)
    v = jnp.var(x, axis=axis, keepdims=True)
    return (x - m) / jnp.sqrt(v + eps)

def _scatter_add(tgt, idx, src, axis=0):
    return tgt.at[idx].add(src)

def _segment_sum(src, seg, n):
    return jax.ops.segment_sum(src, seg, n)
kernel_name = 'mk_decoder_preln_d1_seqx_r8_22faf7'

def setup_inputs(seed: int=0):
    np.random.seed(seed)
    _w = jnp.asarray

    def _rec_inputs():
        import jax
        import jax.numpy as jnp
        _rk = jax.random.key(seed)
        x = -0.0005207 + 1.001 * jax.random.normal(jax.random.fold_in(_rk, 1), (32, 64, 256), jnp.float32)
        _lenS = 64 - jax.random.randint(jax.random.fold_in(_rk, 7), (32,), 0, max(1, 64 // 4) + 1, jnp.int32)
        _lenS2 = 64 - jax.random.randint(jax.random.fold_in(_rk, 8), (32,), 0, max(1, 64 // 4) + 1, jnp.int32)
        _ctx_2048P = jax.random.normal(jax.random.fold_in(_rk, 12), (32, 16, 256), jnp.float32)
        _ctx_2048c = jax.random.dirichlet(jax.random.fold_in(_rk, 512), 0.3 * jnp.ones((16,), jnp.float32), (32, 64))
        _ctx_2048t = jnp.einsum('bsk,bkd->bsd', _ctx_2048c, _ctx_2048P)
        _ctx_2048t = _ctx_2048t * jax.lax.rsqrt(jnp.mean(jnp.square(_ctx_2048t)) + 1e-12) * 0.953939
        ctx_2048 = -5.72187e-05 + 0.999849 * (_ctx_2048t + 0.3 * jax.random.normal(jax.random.fold_in(_rk, 612), (32, 64, 256), jnp.float32))
        _validS = jnp.arange(64)[None, :] < _lenS[:, None]
        _validS2 = jnp.arange(64)[None, :] < _lenS2[:, None]
        _causal = jnp.tril(jnp.ones((64, 64), dtype=bool))
        mask_BxSx4224_bf0 = jnp.logical_not(jnp.ones((32, 64, 528), dtype=bool))
        return (x, ctx_2048, mask_BxSx4224_bf0)
    x, ctx_2048, mask_BxSx4224_bf0 = _rec_inputs()

    def _L0_attn_setup():
        import jax, jax.numpy as jnp
        import numpy as np
        B, S, H, R = (2, 512, 256, 256)
        NB, CW = (16, 4)
        BW = R // NB

        def _block_diag_linear(x, w, b):
            xb = x.reshape(x.shape[0], x.shape[1], NB, BW)
            out = jnp.einsum('bsni,nij->bsnj', xb, w) + b
            return out.reshape(x.shape)

        def _causal_conv1d(x, conv_w, conv_b):
            xp = jnp.pad(x, ((0, 0), (CW - 1, 0), (0, 0)))
            out = conv_b
            for i in range(CW):
                out = out + conv_w[i] * xp[:, i:i + x.shape[1], :]
            return out

        def _rg_lru_scan(x, x_gate_pre, a_gate_pre, a_param):
            gate_x = jax.nn.sigmoid(x_gate_pre)
            gate_a = jax.nn.sigmoid(a_gate_pre)
            log_a = -8.0 * gate_a * jax.nn.softplus(a_param)
            a = jnp.exp(log_a)
            multiplier = jnp.sqrt(-jnp.expm1(2.0 * log_a))
            norm_x = x * gate_x * multiplier

            def combine(c1, c2):
                a1, b1 = c1
                a2, b2 = c2
                return (a1 * a2, a2 * b1 + b2)
            _, h = jax.lax.associative_scan(combine, (a, norm_x), axis=1)
            return h
        key = jax.random.key(seed)
        ks = jax.random.split(key, 9)
        x = jax.random.normal(ks[0], (B, S, H), dtype=jnp.float32)
        W_xy = jax.random.normal(ks[1], (2 * R, H), dtype=jnp.float32) / np.sqrt(H)
        ig_w = jax.random.normal(ks[2], (NB, BW, BW), dtype=jnp.float32) / np.sqrt(BW)
        ig_b = jnp.zeros((NB, BW), dtype=jnp.float32)
        ag_w = jax.random.normal(ks[3], (NB, BW, BW), dtype=jnp.float32) / np.sqrt(BW)
        ag_b = jnp.zeros((NB, BW), dtype=jnp.float32)
        unif = jax.random.uniform(ks[4], (R,), dtype=jnp.float32)
        a_real = 0.5 * jnp.log(unif * (0.999 ** 2 - 0.9 ** 2) + 0.9 ** 2 + 1e-08)
        a_param = jnp.log(jnp.expm1(-a_real))
        conv_w = jax.random.normal(ks[5], (CW, R), dtype=jnp.float32) / np.sqrt(CW * R)
        conv_b = jnp.zeros((R,), dtype=jnp.float32)
        W_resid = 0.02 * jax.random.normal(ks[6], (H, R), dtype=jnp.float32)
        return {'x': x, 'W_xy': W_xy, 'ig_w': ig_w, 'ig_b': ig_b, 'ag_w': ag_w, 'ag_b': ag_b, 'a_param': a_param, 'conv_w': conv_w, 'conv_b': conv_b, 'W_resid': W_resid}
    _L0_attn_all = _L0_attn_setup()
    _L0_attn_in = {k: v for k, v in _L0_attn_all.items() if k in ('W_xy', 'ig_w', 'ig_b', 'ag_w', 'ag_b', 'a_param', 'conv_w', 'conv_b', 'W_resid')}
    del _L0_attn_all

    def _L0_xattn_setup():
        import jax, jax.numpy as jnp
        import numpy as np
        import math
        DIM = 256
        B, Q_LEN, KV_LEN = (8, 128, 512)
        key = jax.random.key(seed)
        ks = jax.random.split(key, 8)
        x = jax.random.normal(ks[0], (B, Q_LEN, DIM), dtype=jnp.float32)
        mask = jnp.zeros((B, Q_LEN, KV_LEN + Q_LEN), dtype=bool)
        k_cache = jax.random.normal(ks[1], (B, KV_LEN, DIM), dtype=jnp.float32)
        v_cache = jax.random.normal(ks[2], (B, KV_LEN, DIM), dtype=jnp.float32)
        scale = 1.0 / math.sqrt(DIM)
        wq = jax.random.normal(ks[3], (DIM, DIM), dtype=jnp.float32) * scale
        wk = jax.random.normal(ks[4], (DIM, DIM), dtype=jnp.float32) * scale
        wv = jax.random.normal(ks[5], (DIM, DIM), dtype=jnp.float32) * scale
        wo = jax.random.normal(ks[6], (DIM, DIM), dtype=jnp.float32) * scale
        return {'x': x, 'mask': mask, 'k_cache': k_cache, 'v_cache': v_cache, 'wq': wq, 'wk': wk, 'wv': wv, 'wo': wo}
    _L0_xattn_all = _L0_xattn_setup()
    _L0_xattn_in = {k: v for k, v in _L0_xattn_all.items() if k in ('wq', 'wk', 'wv', 'wo')}
    del _L0_xattn_all

    def _L0_ffn_setup():
        import jax, jax.numpy as jnp
        import numpy as np
        GOLDEN_CENTER = 1.0 / np.e
        GOLDEN_LOWER = 0.5 - np.log(4.0 / 3.0)
        GOLDEN_UPPER = 0.5

        def _golden_weights(x, Wr, temperature):
            inh = jax.nn.sigmoid(x @ Wr / temperature)
            in_zone = (inh >= GOLDEN_LOWER) & (inh <= GOLDEN_UPPER)
            distance = jnp.abs(inh - GOLDEN_CENTER)
            weights = jnp.exp(-distance / 0.1) * in_zone.astype(x.dtype)
            wsum = jnp.sum(weights, axis=-1, keepdims=True)
            no_expert = wsum < 1e-08
            fb = jnp.exp(-distance / 0.3)
            _, top2 = jax.lax.top_k(fb, 2)
            fb_mask = jnp.sum(jax.nn.one_hot(top2, weights.shape[-1], dtype=x.dtype), axis=-2)
            fb_w = fb * fb_mask
            fb_w = fb_w / jnp.maximum(jnp.sum(fb_w, axis=-1, keepdims=True), 1e-08)
            weights = jnp.where(no_expert, fb_w, weights)
            weights = weights / jnp.maximum(jnp.sum(weights, axis=-1, keepdims=True), 1e-08)
            return weights
        key = jax.random.key(seed)
        ks = jax.random.split(key, 5)
        B, T, D, E, F = (2, 256, 256, 8, 256)
        s_in = 1.0 / np.sqrt(D)
        s_f = 1.0 / np.sqrt(F)
        return {'x': jax.random.normal(ks[0], (B, T, D), dtype=jnp.float32), 'Wg': jax.random.normal(ks[1], (E, D, F), dtype=jnp.float32) * s_in, 'Wu': jax.random.normal(ks[2], (E, D, F), dtype=jnp.float32) * s_in, 'Wd': jax.random.normal(ks[3], (E, F, D), dtype=jnp.float32) * s_f, 'Wr': jax.random.normal(ks[4], (D, E), dtype=jnp.float32) * s_in, 'temperature': jnp.ones((1,), dtype=jnp.float32)}
    _L0_ffn_all = _L0_ffn_setup()
    _L0_ffn_in = {k: v for k, v in _L0_ffn_all.items() if k in ('Wg', 'Wu', 'Wd', 'Wr', 'temperature')}
    del _L0_ffn_all
    return {'x': x, 'ctx_2048': ctx_2048, 'mask_BxSx4224_bf0': mask_BxSx4224_bf0, 'L0_attn_W_xy': _L0_attn_in['W_xy'], 'L0_attn_ig_w': _L0_attn_in['ig_w'], 'L0_attn_ig_b': _L0_attn_in['ig_b'], 'L0_attn_ag_w': _L0_attn_in['ag_w'], 'L0_attn_ag_b': _L0_attn_in['ag_b'], 'L0_attn_a_param': _L0_attn_in['a_param'], 'L0_attn_conv_w': _L0_attn_in['conv_w'], 'L0_attn_conv_b': _L0_attn_in['conv_b'], 'L0_attn_W_resid': _L0_attn_in['W_resid'], 'L0_xattn_wq': _L0_xattn_in['wq'], 'L0_xattn_wk': _L0_xattn_in['wk'], 'L0_xattn_wv': _L0_xattn_in['wv'], 'L0_xattn_wo': _L0_xattn_in['wo'], 'L0_ffn_Wg': _L0_ffn_in['Wg'], 'L0_ffn_Wu': _L0_ffn_in['Wu'], 'L0_ffn_Wd': _L0_ffn_in['Wd'], 'L0_ffn_Wr': _L0_ffn_in['Wr'], 'L0_ffn_temperature': _L0_ffn_in['temperature']}

def reference(x, ctx_2048, mask_BxSx4224_bf0, L0_attn_W_xy, L0_attn_ig_w, L0_attn_ig_b, L0_attn_ag_w, L0_attn_ag_b, L0_attn_a_param, L0_attn_conv_w, L0_attn_conv_b, L0_attn_W_resid, L0_xattn_wq, L0_xattn_wk, L0_xattn_wv, L0_xattn_wo, L0_ffn_Wg, L0_ffn_Wu, L0_ffn_Wd, L0_ffn_Wr, L0_ffn_temperature):
    import jax
    import jax.numpy as jnp

    def _L0_attn_ref(x, W_xy, ig_w, ig_b, ag_w, ag_b, a_param, conv_w, conv_b, W_resid):
        import jax, jax.numpy as jnp
        import numpy as np
        B, S, H, R = (2, 512, 256, 256)
        NB, CW = (16, 4)
        BW = R // NB

        def _block_diag_linear(x, w, b):
            xb = x.reshape(x.shape[0], x.shape[1], NB, BW)
            out = jnp.einsum('bsni,nij->bsnj', xb, w) + b
            return out.reshape(x.shape)

        def _causal_conv1d(x, conv_w, conv_b):
            xp = jnp.pad(x, ((0, 0), (CW - 1, 0), (0, 0)))
            out = conv_b
            for i in range(CW):
                out = out + conv_w[i] * xp[:, i:i + x.shape[1], :]
            return out

        def _rg_lru_scan(x, x_gate_pre, a_gate_pre, a_param):
            gate_x = jax.nn.sigmoid(x_gate_pre)
            gate_a = jax.nn.sigmoid(a_gate_pre)
            log_a = -8.0 * gate_a * jax.nn.softplus(a_param)
            a = jnp.exp(log_a)
            multiplier = jnp.sqrt(-jnp.expm1(2.0 * log_a))
            norm_x = x * gate_x * multiplier

            def combine(c1, c2):
                a1, b1 = c1
                a2, b2 = c2
                return (a1 * a2, a2 * b1 + b2)
            _, h = jax.lax.associative_scan(combine, (a, norm_x), axis=1)
            return h
        xy = jnp.einsum('bsh,rh->bsr', x, W_xy)
        xr, y = jnp.split(xy, 2, axis=-1)
        xc = _causal_conv1d(xr, conv_w, conv_b)
        x_gate_pre = _block_diag_linear(xc, ig_w, ig_b)
        a_gate_pre = _block_diag_linear(xc, ag_w, ag_b)
        h = _rg_lru_scan(xc, x_gate_pre, a_gate_pre, a_param)
        out = jnp.einsum('bsr,hr->bsh', jax.nn.gelu(y, approximate=False) * h, W_resid)
        return out

    def _L0_xattn_ref(x, mask, k_cache, v_cache, wq, wk, wv, wo):
        import jax, jax.numpy as jnp
        import numpy as np
        import math
        DIM = 256
        B, Q_LEN, KV_LEN = (8, 128, 512)
        q = jnp.einsum('bsd,ed->bse', x, wq)
        k_new = jnp.einsum('bsd,ed->bse', x, wk)
        v_new = jnp.einsum('bsd,ed->bse', x, wv)
        k = jnp.concatenate([k_cache, k_new], axis=1)
        v = jnp.concatenate([v_cache, v_new], axis=1)
        scale = 1.0 / math.sqrt(q.shape[-1])
        scores = jnp.einsum('bqd,bkd->bqk', q, k) * scale
        attn = jax.nn.softmax(scores, axis=-1)
        out = jnp.einsum('bqk,bkd->bqd', attn, v)
        return jnp.einsum('bqd,ed->bqe', out, wo)

    def _L0_ffn_ref(x, Wg, Wu, Wd, Wr, temperature):
        import jax, jax.numpy as jnp
        import numpy as np
        GOLDEN_CENTER = 1.0 / np.e
        GOLDEN_LOWER = 0.5 - np.log(4.0 / 3.0)
        GOLDEN_UPPER = 0.5

        def _golden_weights(x, Wr, temperature):
            inh = jax.nn.sigmoid(x @ Wr / temperature)
            in_zone = (inh >= GOLDEN_LOWER) & (inh <= GOLDEN_UPPER)
            distance = jnp.abs(inh - GOLDEN_CENTER)
            weights = jnp.exp(-distance / 0.1) * in_zone.astype(x.dtype)
            wsum = jnp.sum(weights, axis=-1, keepdims=True)
            no_expert = wsum < 1e-08
            fb = jnp.exp(-distance / 0.3)
            _, top2 = jax.lax.top_k(fb, 2)
            fb_mask = jnp.sum(jax.nn.one_hot(top2, weights.shape[-1], dtype=x.dtype), axis=-2)
            fb_w = fb * fb_mask
            fb_w = fb_w / jnp.maximum(jnp.sum(fb_w, axis=-1, keepdims=True), 1e-08)
            weights = jnp.where(no_expert, fb_w, weights)
            weights = weights / jnp.maximum(jnp.sum(weights, axis=-1, keepdims=True), 1e-08)
            return weights
        weights = _golden_weights(x, Wr, temperature)
        gate = jnp.einsum('btd,edf->betf', x, Wg)
        up = jnp.einsum('btd,edf->betf', x, Wu)
        h = jax.nn.silu(gate) * up
        e_out = jnp.einsum('betf,efd->betd', h, Wd)
        out = jnp.einsum('bte,betd->btd', weights, e_out)
        return out
    x = x + _L0_attn_ref(_layernorm(x, axis=-1), L0_attn_W_xy, L0_attn_ig_w, L0_attn_ig_b, L0_attn_ag_w, L0_attn_ag_b, L0_attn_a_param, L0_attn_conv_w, L0_attn_conv_b, L0_attn_W_resid)
    x = x + _L0_xattn_ref(_layernorm(x, axis=-1), mask_BxSx4224_bf0, ctx_2048, ctx_2048, L0_xattn_wq, L0_xattn_wk, L0_xattn_wv, L0_xattn_wo)
    x = x + _L0_ffn_ref(_layernorm(x, axis=-1), L0_ffn_Wg, L0_ffn_Wu, L0_ffn_Wd, L0_ffn_Wr, L0_ffn_temperature)
    return x

_drawn_inputs = setup_inputs


def setup_inputs(seed=0):
    import zlib

    import numpy as np

    out = dict(_drawn_inputs(seed))
    spreads = {'L0_attn_ig_b': (0.0, 0.642), 'L0_attn_ag_b': (0.0, 2.0), 'L0_attn_conv_b': (0.0, 0.1)}
    factors = {'L0_attn_ig_w': 4.917, 'L0_attn_ag_w': 21.383}
    for name, (base, spread) in spreads.items():
        noise = np.random.default_rng([zlib.crc32(name.encode()), seed]).standard_normal(out[name].shape)
        drawn = base * np.exp(spread * noise) if base else spread * noise
        out[name] = jnp.asarray(drawn.astype(out[name].dtype))
    for name, factor in factors.items():
        out[name] = (out[name] * factor).astype(out[name].dtype)
    return out
```

```python
from contextlib import ExitStack

import concourse.bass as bass
from concourse import mybir

ALU = mybir.AluOpType
ACT = mybir.ActivationFunctionType
AX = mybir.AxisListType
F32 = mybir.dt.float32
F32R = mybir.dt.float32r

P = 128
SEQ = 64
D = 256
C = D // P
BLK = 512
TPB = BLK // P
SPB = BLK // SEQ
CW = 4
PADDED = SEQ + CW - 1
SCALE = 1.0 / 16.0
EPS = 1e-5
GOLDEN_CENTER = 0.36787944117144233
GOLDEN_LOWER = 0.21231792754821915
GOLDEN_UPPER = 0.5
ATANH_TERMS = 9


class Tally:

    def __init__(self, sem, per_block):
        self.sem, self.per_block = sem, per_block

    def start(self, eng):
        eng.sem_inc(self.sem, 1)

    def wait(self, eng, b, k):
        eng.wait_ge(self.sem, b * self.per_block + (k + 1))

    def wait_apart(self, eng, b, k, passed):
        self.wait(eng, b, k)
        eng.sem_inc(passed, 1)


def decoder_kernel(nc, x, ctx_t, w_stage1, w_stage2, channel_vecs, w_experts, temperature, out):
    tokens = x.shape[0]
    NB = tokens // BLK
    NT = tokens // P
    E = w_experts.shape[0]
    WE = w_experts.shape[2]

    x_tiles = x.rearrange("(t p) d -> p t d", p=P)
    out_tiles = out.rearrange("(t p) d -> p t d", p=P)

    with ExitStack() as stack:
        def sb(name, shape, dt=F32):
            return stack.enter_context(nc.sbuf_tensor(name, shape, dt))

        def sem(name):
            return stack.enter_context(nc.semaphore(name))

        def tally(name, per_block):
            return Tally(sem(name), per_block)

        x_all = sb("x_all", [P, NT, D])
        x3t_hi = sb("x3t_hi", [P, C, tokens], F32R)
        x3t_lo = sb("x3t_lo", [P, C, tokens], F32R)
        logits = sb("logits", [P, NT, E])
        combine = sb("combine", [P, NT, E])
        ident = sb("ident", [P, P])
        w1 = sb("w1", [P, C * 2 * D + 2 * C * P + C * D])
        w_xy = w1[:, 0:1024].rearrange("p (k n) -> p k n", k=C)
        w_gates = w1[:, 1024:1536].rearrange("p (g c n) -> p g c n", g=2, c=C)
        w_resid = w1[:, 1536:2048].rearrange("p (k n) -> p k n", k=C)
        w2 = sb("w2", [P, 4 * C * D + C * E])
        w_q, w_k, w_o, w_v = (w2[:, 512 * n:512 * n + 512].rearrange("p (k n) -> p k n", k=C) for n in range(4))
        w_r = w2[:, 2048:2048 + C * E].rearrange("p (k n) -> p k n", k=C)
        w_vo = sb("w_vo", [P, C, D])
        vec = sb("vec", [P, C, 8])
        decay = sb("decay", [P, C])
        neg_decay = sb("neg_decay", [P, C])
        sp = sb("sp", [P, 5, C])
        temp = sb("temp", [P, 1])
        inv_temp = sb("inv_temp", [P, 1])
        exponent = sb("exponent", [P, TPB])
        earlier = sb("earlier", [P, E * E])
        w_raw = sb("w_raw", [P, WE])
        w_hi = sb("w_hi", [P, 2, WE], F32R)
        w_lo = sb("w_lo", [P, 2, WE], F32R)
        stats = sb("stats", [P, 3, TPB, 6])
        mv = sb("mv", [P, 3, TPB, 2])
        var_eps = sb("var_eps", [P, 3, TPB])
        rstd = sb("rstd", [P, 3, TPB])
        xn1 = sb("xn1", [P, TPB, D])
        x1t = sb("x1t", [P, C, BLK])
        xr_pad = sb("xr_pad", [P, C, SPB, PADDED])
        gelu_y = sb("gelu_y", [P, C, BLK])
        xc = sb("xc", [P, C, BLK])
        sig = sb("sig", [P, 2, C, BLK])
        gated = sb("gated", [P, C, BLK])
        a = sb("a", [P, C, BLK])
        tnh = sb("tnh", [P, C, BLK])
        mult = sb("mult", [P, C, BLK])
        h = sb("h", [P, C, BLK])
        xn2 = sb("xn2", [P, TPB, D])
        x2t = sb("x2t", [P, C, BLK])
        ctxt = sb("ctxt", [P, C, BLK])
        qt = sb("qt", [P, C, BLK])
        knt = sb("knt", [P, C, BLK])
        v_ctx = sb("v_ctx", [P, TPB, D])
        v_new = sb("v_new", [P, TPB, D])
        smax = sb("smax", [P, TPB])
        ssum = sb("ssum", [P, TPB])
        sinv = sb("sinv", [P, TPB])
        probs = sb("probs", [P, TPB, 2, 2, SEQ])
        probs_t = sb("probs_t", [P, TPB, 2, P])
        xn3 = sb("xn3", [P, TPB, D])
        x3t = sb("x3t", [P, C, BLK])
        h_hi = sb("h_hi", [P, 2, C, BLK], F32R)
        h_lo = sb("h_lo", [P, 2, C, BLK], F32R)
        silu_g = sig
        h_raw = [gated, a]

        banks = [stack.enter_context(nc.psum_tensor(f"bank{n}", [P, BLK], F32)) for n in range(8)]
        pT = banks[0:2]
        pA = banks[2:4]
        pB = banks[4:6]
        pS = banks[6:8]

        s_x0 = sem("x_block0_in")
        s_xrest = sem("x_rest_in")
        s_w1 = sem("w1_in")
        s_w2 = sem("w2_in")
        s_vec = sem("vec_in")
        s_out = sem("out_written")
        s_ctx = sem("ctx_in")
        s_ident = sem("ident_ready")
        s_const = sem("const_ready")
        s_sp_act = sem("softplus_act")
        s_setup = sem("dve_setup")
        s_wvo = sem("wvo_ready")
        s_wvo_sb = sem("wvo_copied")
        s_wraw = sem("expert_weights_in")
        dve_passed = sem("dve_waits_passed")
        pool_passed = sem("pool_waits_passed")
        ln1_stats = tally("ln1_stats", TPB + 2)
        ln1_rstd = tally("ln1_rstd", 1)
        ln1_done = tally("ln1_done", TPB)
        ln2_stats = tally("ln2_stats", TPB + 2)
        ln2_rstd = tally("ln2_rstd", 1)
        ln2_done = tally("ln2_done", TPB)
        ln3_stats = tally("ln3_stats", TPB + 2)
        ln3_rstd = tally("ln3_rstd", 1)
        ln3_done = tally("ln3_done", TPB)
        t1_done = tally("t1_done", C)
        t1_taken = tally("t1_taken", C)
        t2_done = tally("t2_done", C)
        t2_taken = tally("t2_taken", C)
        t3_done = tally("t3_done", C)
        t3_taken = tally("t3_taken", C)
        tp_done = tally("probs_transposed", 2)
        tp_taken = tally("probs_t_taken", 2)
        xy_done = tally("xy_done", 4)
        xy_taken = tally("xy_taken", 4)
        conv_step = tally("conv_step", C * CW)
        gate_done = tally("gate_done", 4)
        gate_taken = tally("gate_taken", 4)
        gated_done = tally("gated_done", C)
        decay_done = tally("decay_done", 2 * C)
        square_done = tally("square_done", C)
        multsq_done = tally("multsq_done", C)
        sqrt_done = tally("sqrt_done", C)
        scan_step = tally("scan_step", 4 * C)
        resid_done = tally("resid_done", 2)
        x1_done = tally("x1_done", 2)
        qk_done = tally("qk_done", 4)
        qk_taken = tally("qk_taken", 4)
        v_done = tally("v_done", 4)
        v_taken = tally("v_taken", 4)
        score_done = tally("score_done", 2)
        max_done = tally("max_done", 4)
        sub_done = tally("sub_done", 4)
        exp_done = tally("exp_done", 2)
        sum_done = tally("sum_done", 2)
        pv_done = tally("pv_done", 2)
        x2_done = tally("x2_done", TPB)
        router_done = tally("router_done", 1)
        router_taken = tally("router_taken", 1)
        split3 = tally("x3_split", 2 * C)
        gu_done = tally("gate_up_done", C)
        silu_done = tally("silu_done", C)
        hraw_done = tally("h_done", C)
        hhi_done = tally("h_hi_done", C)
        hlo_done = tally("h_lo_done", C)
        down_done = tally("down_done", 2)
        acc_done = tally("acc_done", TPB)
        whi_done = tally("w_hi_done", 1)
        wlo_done = tally("w_lo_done", 1)
        s_route = sem("route_step")
        s_route_act = sem("route_act")

        block = stack.enter_context(nc.Block())
        STEPS = NB

        def gate_bank(f):
            return banks[2 * f]

        def up_bank(f):
            return banks[2 * f + 1]

        def down_bank(half):
            return banks[4 + half]

        def small(n, width):
            return xc[:].rearrange("p c t -> p (c t)")[:, 128 * n:128 * n + width]

        inside, dist, zone, golden, fallback, rank = (
            small(n, NT * E).rearrange("p (t e) -> p t e", t=NT) for n in range(6))
        gsum, none_in, fsum = (small(6, 3 * NT)[:, NT * n:NT * n + NT] for n in range(3))
        above, equal = (m[:].rearrange("p c t -> p (c t)").rearrange("p (t i j) -> p t i j", t=NT, i=E)
                        for m in (tnh, mult))
        R_LOGIT, R_DIST = 1, 3
        SETUP_STEPS = 7 + ATANH_TERMS + 4

        @block.sync
        def _(sp_eng):
            sp_eng.dma_start(x_all[:, 0:TPB, :], x_tiles[:, 0:TPB, :]).then_inc(s_x0, 16)
            sp_eng.dma_start(w1[:], w_stage1).then_inc(s_w1, 16)
            sp_eng.dma_start(vec[:], channel_vecs).then_inc(s_vec, 16)
            sp_eng.dma_start(temp[:], temperature.partition_broadcast(P)).then_inc(s_vec, 16)
            sp_eng.dma_start(ctxt[:], ctx_t[0]).then_inc(s_ctx, 16)
            sp_eng.dma_start(w2[:], w_stage2).then_inc(s_w2, 16)
            sp_eng.dma_start(x_all[:, TPB:, :], x_tiles[:, TPB:, :]).then_inc(s_xrest, 16)
            sp_eng.dma_start(w_raw[:], w_experts[0]).then_inc(s_wraw, 16)
            with sp_eng.Fori(1, NB) as b:
                v_done.wait(sp_eng, b, 0)
                score_done.wait(sp_eng, b, 0)
                sp_eng.dma_start(ctxt[:], ctx_t[bass.ds(b, 1)].rearrange("o p c t -> (o p) c t")).then_inc(s_ctx, 16)
            with sp_eng.Fori(1, E) as e:
                whi_done.wait(sp_eng, e, 0)
                wlo_done.wait(sp_eng, e, 0)
                sp_eng.dma_start(w_raw[:], w_experts[bass.ds(e, 1)].rearrange("o p n -> (o p) n")).then_inc(s_wraw, 16)
            for b in range(NB):
                acc_done.wait(sp_eng, (E - 1) * STEPS + b, TPB)
                sp_eng.dma_start(out_tiles[:, TPB * b:TPB * b + TPB, :],
                                 x_all[:, TPB * b:TPB * b + TPB, :]).then_inc(s_out, 16)
            sp_eng.wait_ge(s_out, 16 * NB)

        @block.gpsimd
        def _(pool):
            for t in (ln1_rstd, ln2_rstd, ln3_rstd, gated_done, split3, hlo_done, whi_done, wlo_done):
                t.start(pool)
            pool.memset(ident[:], 0.0).then_inc(s_ident, 1)
            pool.wait_ge(s_ident, 1)
            pool.affine_select(out=ident[:], in_=ident[:], compare_op=ALU.not_equal, fill=1.0, base=0,
                               pattern=[[-1, P]], channel_multiplier=1).then_inc(s_ident, 1)
            pool.memset(exponent[:], -0.5).then_inc(s_const, 1)
            pool.memset(xr_pad[:], 0.0).then_inc(s_const, 1)
            pool.memset(earlier[:], 1.0).then_inc(s_const, 1)
            pool.wait_ge(s_const, 3)
            pool.affine_select(out=earlier[:], in_=earlier[:], compare_op=ALU.is_gt, fill=0.0, base=0,
                               pattern=[[1, E], [-1, E]], channel_multiplier=0).then_inc(s_const, 1)
            pool.memset(probs[:], 0.0).then_inc(s_const, 1)

            def inverse_deviation(b, n, stats_done, rstd_done):
                stats_done.wait(pool, b, TPB + 2)
                pool.tensor_tensor(rstd[:, n, :], var_eps[:, n, :], exponent[:], ALU.pow).then_inc(rstd_done.sem, 1)

            def split_expert(e, parity):
                pool.wait_ge(s_wraw, e * 16 + 16)
                pool.sem_inc(pool_passed, 1)
                pool.tensor_copy(w_hi[:, parity, :], w_raw[:]).then_inc(whi_done.sem, 1)
                whi_done.wait(pool, e, 1)
                pool.tensor_tensor(w_lo[:, parity, :], w_raw[:], w_hi[:, parity, :].bitcast(F32),
                                   ALU.subtract).then_inc(wlo_done.sem, 1)

            def stage1(b):
                inverse_deviation(b, 0, ln1_stats, ln1_rstd)
                for c in range(C):
                    conv_step.wait(pool, b, CW * (c + 1))
                    gate_taken.wait(pool, b, 2 * c + 1)
                    scan_step.wait(pool, b, 0)
                    pool.tensor_tensor(gated[:, c, :], xc[:, c, :], sig[:, 0, c, :], ALU.mult)\
                        .then_inc(gated_done.sem, 1)

            def split_x3(b):
                for c in range(C):
                    t3_taken.wait_apart(pool, b, c + 1, pool_passed)
                    dst = x3t_hi[:, c, bass.ds(b * BLK, BLK)]
                    pool.tensor_copy(dst, x3t[:, c, :]).then_inc(split3.sem, 1)
                for c in range(C):
                    split3.wait(pool, b, c + 1)
                    cols = bass.ds(b * BLK, BLK)
                    pool.tensor_tensor(x3t_lo[:, c, cols], x3t[:, c, :], x3t_hi[:, c, cols].bitcast(F32),
                                       ALU.subtract).then_inc(split3.sem, 1)

            stage1(0)
            inverse_deviation(0, 1, ln2_stats, ln2_rstd)
            split_expert(0, 0)
            with pool.Fori(1, NB) as i:
                stage1(i)
                inverse_deviation(i - 1, 2, ln3_stats, ln3_rstd)
                inverse_deviation(i, 1, ln2_stats, ln2_rstd)
                split_x3(i - 1)
            split_expert(1, 1)
            inverse_deviation(NB - 1, 2, ln3_stats, ln3_rstd)
            split_x3(NB - 1)

            def split_h(n, parity):
                for f in range(C):
                    hraw_done.wait(pool, n, f + 1)
                    hhi_done.wait(pool, n, f + 1)
                    pool.tensor_tensor(h_lo[:, parity, f, :], h_raw[parity][:, f, :],
                                       h_hi[:, parity, f, :].bitcast(F32), ALU.subtract).then_inc(hlo_done.sem, 1)

            def next_weights(e, parity):
                down_done.wait(pool, (e - 1) * STEPS - 1, 2)
                split_expert(e, parity)

            split_h(0, 0)
            with pool.Fori(0, E // 2 - 1) as pair:
                for j in range(1, 2 * STEPS + 1):
                    split_h(pair * 2 * STEPS + j, j % 2)
                    if j % STEPS == 0:
                        next_weights(pair * 2 + 1 + j // STEPS, j // STEPS - 1)
            for j in range(1, 2 * STEPS):
                split_h((E - 2) * STEPS + j, j % 2)

        @block.scalar
        def _(act):
            for t in (t1_taken, t2_taken, t3_taken, tp_taken, xy_taken, gate_taken, decay_done, square_done,
                      sqrt_done, qk_taken, v_taken, exp_done, silu_done, hhi_done):
                t.start(act)
            act.wait_ge(s_setup, 1)
            act.activation(sp[:, 1, :], sp[:, 0, :], ACT.Exp, scale=-1.0).then_inc(s_sp_act, 1)
            def copy_out(b, psum, dst, ready, k, taken):
                ready.wait(act, b, k + 1)
                act.activation(dst, psum, ACT.Copy).then_inc(taken.sem, 1)

            def stage1_in(b):
                for c in range(C):
                    copy_out(b, pT[c][:], x1t[:, c, :], t1_done, c, t1_taken)
                act.wait_ge(s_const, 2)
                for c in range(C):
                    if c == 0:
                        conv_step.wait(act, b, 0)
                    copy_out(b, pA[c][:].rearrange("p (s t) -> p s t", s=SPB), xr_pad[:, c, :, CW - 1:PADDED],
                             xy_done, c, xy_taken)
                scan_step.wait(act, b, 0)
                for c in range(C):
                    xy_done.wait(act, b, C + c + 1)
                    act.activation(gelu_y[:, c, :], pA[c][:], ACT.Gelu).then_inc(xy_taken.sem, 1)

            def stage1_gates(b):
                gated_done.wait(act, b, 0)
                decay_done.wait(act, b, 0)
                for c in range(C):
                    for g in range(2):
                        gate_done.wait(act, b, 2 * c + g + 1)
                        act.activation(sig[:, g, c, :], pA[g][:], ACT.Sigmoid,
                                       bias=vec[:, c, 5 + g:6 + g]).then_inc(gate_taken.sem, 1)

            def stage1_decay(b):
                act.wait_ge(s_setup, SETUP_STEPS)
                scan_step.wait(act, b, 0)
                multsq_done.wait(act, b, 0)
                gate_taken.wait(act, b, 4)
                for c in range(C):
                    act.activation(a[:, c, :], sig[:, 1, c, :], ACT.Exp,
                                   scale=neg_decay[:, c:c + 1]).then_inc(decay_done.sem, 1)
                for c in range(C):
                    act.activation(tnh[:, c, :], sig[:, 1, c, :], ACT.Tanh,
                                   scale=decay[:, c:c + 1]).then_inc(decay_done.sem, 1)
                for c in range(C):
                    decay_done.wait(act, b, c + 1)
                    act.activation(mult[:, c, :], a[:, c, :], ACT.Square).then_inc(square_done.sem, 1)

            def stage1_sqrt(b):
                for c in range(C):
                    multsq_done.wait(act, b, c + 1)
                    act.activation(mult[:, c, :], tnh[:, c, :], ACT.Sqrt).then_inc(sqrt_done.sem, 1)

            def stage2_in(b):
                for c in range(C):
                    copy_out(b, pT[c][:], x2t[:, c, :], t2_done, c, t2_taken)
                for n in range(C):
                    copy_out(b, pB[n][:], qt[:, n, :], qk_done, n, qk_taken)
                for n in range(C):
                    copy_out(b, pB[n][:], knt[:, n, :], qk_done, C + n, qk_taken)

            def stage2_values(b):
                for n in range(2):
                    copy_out(b, pB[n][:].rearrange("p (t d) -> p t d", t=2), v_ctx[:, 2 * n:2 * n + 2, :],
                             v_done, n, v_taken)
                for n in range(2):
                    copy_out(b, pB[n][:].rearrange("p (t d) -> p t d", t=2), v_new[:, 2 * n:2 * n + 2, :],
                             v_done, 2 + n, v_taken)

            def stage2_exp(b):
                for s in range(2):
                    sub_done.wait(act, b, 4)
                    part = probs[SEQ * s:SEQ * s + SEQ, :, :, s, :]
                    act.activation(part, part, ACT.Exp, scale=SCALE).then_inc(exp_done.sem, 1)

            def stage2_out(b):
                for n in range(2):
                    copy_out(b, pT[n][:].rearrange("p (t k q) -> p t k q", t=2, k=2),
                             probs_t[:, 2 * n:2 * n + 2, :, :], tp_done, n, tp_taken)

            def stage2_x3(b):
                split3.wait(act, b, 0)
                for c in range(C):
                    copy_out(b, pT[c][:], x3t[:, c, :], t3_done, c, t3_taken)

            stage1_in(0)
            for k in range(C):
                act.wait_ge(s_wvo, k + 1)
                act.activation(w_vo[:, k, :], pS[k][:, 0:D], ACT.Copy).then_inc(s_wvo_sb, 1)
            stage1_gates(0)
            stage1_decay(0)
            stage1_sqrt(0)
            with act.Fori(1, NB) as i:
                stage2_in(i - 1)
                stage1_in(i)
                stage2_values(i - 1)
                stage1_gates(i)
                stage1_decay(i)
                stage2_exp(i - 1)
                stage1_sqrt(i)
                stage2_out(i - 1)
                stage2_x3(i - 1)
            stage2_in(NB - 1)
            stage2_values(NB - 1)
            stage2_exp(NB - 1)
            stage2_out(NB - 1)
            stage2_x3(NB - 1)

            act.wait_ge(s_route, R_LOGIT)
            act.activation(inside, inside, ACT.Sigmoid).then_inc(s_route_act, 1)
            act.wait_ge(s_route, R_DIST)
            act.activation(golden, dist, ACT.Exp, scale=-10.0).then_inc(s_route_act, 1)
            act.activation(fallback, dist, ACT.Exp, scale=-1.0 / 0.3).then_inc(s_route_act, 1)

            with act.Fori(0, E // 2) as pair:
                for j in range(2 * STEPS):
                    n = pair * 2 * STEPS + j
                    for f in range(C):
                        gu_done.wait(act, n, f + 1)
                        act.activation(silu_g[:, j % 2, f, :], gate_bank(f)[:], ACT.Silu).then_inc(silu_done.sem, 1)
                    for f in range(C):
                        hraw_done.wait(act, n, f + 1)
                        act.activation(h_hi[:, j % 2, f, :], h_raw[j % 2][:, f, :], ACT.Copy)\
                            .then_inc(hhi_done.sem, 1)

        @block.tensor
        def _(pe):
            for t in (t1_done, t2_done, t3_done, tp_done, xy_done, gate_done, resid_done, qk_done, v_done,
                      score_done, pv_done, router_done, gu_done, down_done):
                t.start(pe)

            def product(dst, lhs, rhs, done=None):
                for k in range(C):
                    last = pe.matmul(dst, lhs(k), rhs(k), start=(k == 0), stop=(k == C - 1))
                if done is not None:
                    last.then_inc(done.sem, 1)

            def transposes(b, src, ready, done):
                for c in range(C):
                    for t in range(TPB):
                        if c == 0:
                            ready.wait(pe, b, t + 1)
                        last = pe.transpose(pT[c][:, P * t:P * t + P], src[:, t, P * c:P * c + P], ident[:])
                    last.then_inc(done.sem, 1)

            def t1(b):
                transposes(b, xn1, ln1_done, t1_done)

            def xy(b):
                t1_taken.wait(pe, b, C)
                for n in range(2 * C):
                    if n < C:
                        x1_done.wait(pe, b, 0)
                    else:
                        xy_taken.wait(pe, b, n - C + 1)
                    product(pA[n % C][:], lambda k: w_xy[:, k, P * n:P * n + P], lambda k: x1t[:, k, :], xy_done)

            def gates(b):
                for c in range(C):
                    conv_step.wait(pe, b, CW * (c + 1))
                    for g in range(2):
                        if c == 0:
                            xy_taken.wait(pe, b, C + g + 1)
                        else:
                            gate_taken.wait(pe, b, g + 1)
                        pe.matmul(pA[g][:], w_gates[:, g, c, :], xc[:, c, :], start=True, stop=True)\
                            .then_inc(gate_done.sem, 1)

            def resid(b):
                scan_step.wait(pe, b, 4 * C)
                gate_taken.wait(pe, b, 4)
                for t in range(TPB):
                    dst = pA[t // 2][:, D * (t % 2):D * (t % 2) + D]
                    product(dst, lambda k: h[:, k, P * t:P * t + P], lambda k: w_resid[:, k, :],
                            resid_done if t % 2 else None)

            def t2(b):
                t3_taken.wait(pe, b, 0)
                transposes(b, xn2, ln2_done, t2_done)

            def qk(b):
                t2_taken.wait(pe, b, C)
                for n in range(2 * C):
                    w = w_q if n < C else w_k
                    if n < C:
                        v_taken.wait(pe, b, 0)
                        router_taken.wait(pe, b, 0)
                    else:
                        qk_taken.wait(pe, b, n - C + 1)
                    product(pB[n % C][:], lambda k: w[:, k, P * (n % C):P * (n % C) + P],
                            lambda k: x2t[:, k, :], qk_done)

            def values(b):
                pe.wait_ge(s_ctx, b * 16 + 16)
                for n in range(4):
                    src, w = (ctxt, w_o) if n < 2 else (x2t, w_vo)
                    if n < 2:
                        qk_taken.wait(pe, b, C + n + 1)
                    else:
                        v_taken.wait(pe, b, n - 1)
                    for u in range(2):
                        t = 2 * (n % 2) + u
                        product(pB[n % 2][:, D * u:D * u + D], lambda k: src[:, k, P * t:P * t + P],
                                lambda k: w[:, k, :], v_done if u else None)

            def scores(b):
                qk_taken.wait(pe, b, 2 * C)
                x2_done.wait(pe, b, 0)
                for t in range(TPB):
                    pair = slice(P * t, P * t + P)
                    for m, keys in enumerate((ctxt, knt)):
                        at = D * (t % 2) + P * m
                        for k in range(C):
                            last = pe.matmul(pS[t // 2][:, at:at + P], qt[:, k, pair], keys[:, k, pair],
                                             start=(k == 0), stop=(k == C - 1))
                    if t % 2:
                        last.then_inc(score_done.sem, 1)

            def probs_transpose(b):
                exp_done.wait(pe, b, 2)
                for t in range(TPB):
                    for m in range(2):
                        at = D * (t % 2) + P * m
                        last = pe.transpose(pT[t // 2][:, at:at + P],
                                            probs[:, t, m, :, :].rearrange("p s k -> p (s k)"), ident[:])
                    if t % 2:
                        last.then_inc(tp_done.sem, 1)

            def attend(b):
                sub_done.wait(pe, b, 4)
                v_taken.wait(pe, b, 4)
                for t in range(TPB):
                    tp_taken.wait(pe, b, t // 2 + 1)
                    dst = pS[t // 2][:, D * (t % 2):D * (t % 2) + D]
                    for m, v in enumerate((v_ctx, v_new)):
                        last = pe.matmul(dst, probs_t[:, t, m, :], v[:, t, :], start=(m == 0), stop=(m == 1))
                    if t % 2:
                        last.then_inc(pv_done.sem, 1)

            def t3(b):
                tp_taken.wait(pe, b, 2)
                transposes(b, xn3, ln3_done, t3_done)

            def router(b):
                t3_taken.wait(pe, b, C)
                v_taken.wait(pe, b, 4)
                router_taken.wait(pe, b, 0)
                for t in range(TPB):
                    product(pB[0][:, E * t:E * t + E], lambda k: x3t[:, k, P * t:P * t + P], lambda k: w_r[:, k, :],
                            router_done if t == TPB - 1 else None)

            pe.wait_ge(s_ident, 2)
            transposes(0, xn1, ln1_done, t1_done)
            pe.wait_ge(s_w1, 16)
            xy(0)
            pe.wait_ge(s_w2, 16)
            for k in range(C):
                for j in range(C):
                    last = pe.matmul(pS[k][:, 0:D], w_v[:, j, P * k:P * k + P], w_o[:, j, :],
                                     start=(j == 0), stop=(j == C - 1))
                last.then_inc(s_wvo, 1)
            gates(0)
            resid(0)
            pe.wait_ge(s_wvo_sb, C)
            with pe.Fori(1, NB) as i:
                t2(i - 1)
                qk(i - 1)
                t1(i)
                xy(i)
                values(i - 1)
                gates(i)
                scores(i - 1)
                probs_transpose(i - 1)
                attend(i - 1)
                resid(i)
                t3(i - 1)
                router(i - 1)
            t2(NB - 1)
            qk(NB - 1)
            values(NB - 1)
            scores(NB - 1)
            probs_transpose(NB - 1)
            attend(NB - 1)
            t3(NB - 1)
            router(NB - 1)

            def split_product(terms, dst, done=None):
                n = 3 * len(terms)
                i = 0
                for lh, ll, rh, rl in terms:
                    for p, q in ((lh, rh), (lh, rl), (ll, rh)):
                        last = pe.matmul(dst, p, q, start=(i == 0), stop=(i == n - 1))
                        i += 1
                if done is not None:
                    last.then_inc(done.sem, 1)

            def gate_up(n, e, j):
                par, cols = (j // STEPS) % 2, slice(BLK * (j % STEPS), BLK * (j % STEPS) + BLK)
                if j % STEPS == 0:
                    wlo_done.wait(pe, e, 1)
                for f in range(C):
                    if j:
                        hraw_done.wait(pe, n - 1, f + 1)
                    for which, dst in ((0, gate_bank(f)), (1, up_bank(f))):
                        terms = []
                        for k in range(C):
                            at = (which * C + k) * D + P * f
                            terms.append((w_hi[:, par, at:at + P], w_lo[:, par, at:at + P],
                                          x3t_hi[:, k, cols], x3t_lo[:, k, cols]))
                        split_product(terms, dst[:], gu_done if which else None)

            def down(n, j):
                par = (j // STEPS) % 2
                acc_done.wait(pe, n, 0)
                hlo_done.wait(pe, n, C)
                for t in range(TPB):
                    terms = []
                    for f in range(C):
                        at = (2 * C + f) * D
                        tile = slice(P * t, P * t + P)
                        terms.append((h_hi[:, j % 2, f, tile], h_lo[:, j % 2, f, tile],
                                      w_hi[:, par, at:at + D], w_lo[:, par, at:at + D]))
                    split_product(terms, down_bank(t // 2)[:, D * (t % 2):D * (t % 2) + D],
                                  down_done if t % 2 else None)

            split3.wait(pe, NB - 1, 2 * C)
            router_taken.wait(pe, NB - 1, 1)
            x2_done.wait(pe, NB - 1, TPB)
            gate_up(0, 0, 0)
            with pe.Fori(0, E // 2 - 1) as pair:
                for j in range(2 * STEPS):
                    n = pair * 2 * STEPS + j
                    gate_up(n + 1, pair * 2 + (j + 1) // STEPS, j + 1)
                    down(n, j)
            for j in range(2 * STEPS):
                n = (E - 2) * STEPS + j
                if j < 2 * STEPS - 1:
                    gate_up(n + 1, E - 2 + (j + 1) // STEPS, j + 1)
                down(n, j)

        @block.vector
        def _(dve):
            for t in (ln1_stats, ln1_done, ln2_stats, ln2_done, ln3_stats, ln3_done, conv_step, multsq_done,
                      scan_step, x1_done, max_done, sub_done, sum_done, x2_done, router_taken, hraw_done, acc_done):
                t.start(dve)

            def layernorm(b, n, xn, stats_done, rstd_done, done):
                def tile(t):
                    return x_all[:, bass.ds(b * TPB + t, 1), :].rearrange("p o d -> p (o d)")
                for t in range(TPB):
                    dve.bn_stats(stats[:, n, t, :], tile(t)).then_inc(stats_done.sem, 1)
                stats_done.wait_apart(dve, b, TPB, dve_passed)
                for t in range(TPB):
                    ins = dve.bn_aggr(mv[:, n, t, :], stats[:, n, t, :])
                ins.then_inc(stats_done.sem, 1)
                stats_done.wait(dve, b, TPB + 1)
                dve.tensor_scalar(var_eps[:, n, :], mv[:, n, :, 1], EPS, None, ALU.add).then_inc(stats_done.sem, 1)
                rstd_done.wait(dve, b, 1)
                for t in range(TPB):
                    dve.tensor_scalar(xn[:, t, :], tile(t), mv[:, n, t, 0:1], rstd[:, n, t:t + 1],
                                      ALU.subtract, ALU.mult).then_inc(done.sem, 1)

            def ln1(b):
                t1_done.wait_apart(dve, b, 0, dve_passed)
                layernorm(b, 0, xn1, ln1_stats, ln1_rstd, ln1_done)

            def ln2(b):
                t2_done.wait(dve, b, 0)
                x1_done.wait_apart(dve, b, 2, dve_passed)
                layernorm(b, 1, xn2, ln2_stats, ln2_rstd, ln2_done)

            def ln3(b):
                t3_done.wait(dve, b, 0)
                x2_done.wait_apart(dve, b, TPB, dve_passed)
                layernorm(b, 2, xn3, ln3_stats, ln3_rstd, ln3_done)

            def conv(b):
                gate_done.wait(dve, b, 0)
                gated_done.wait(dve, b, 0)
                for c in range(C):
                    xy_taken.wait(dve, b, c + 1)
                    view = xc[:, c, :].rearrange("p (s t) -> p s t", s=SPB)
                    for i in range(CW):
                        src = xr_pad[:, c, :, i:i + SEQ]
                        if i == 0:
                            ins = dve.tensor_scalar(view, src, vec[:, c, 0:1], vec[:, c, 4:5], ALU.mult, ALU.add)
                        else:
                            conv_step.wait(dve, b, CW * c + i)
                            ins = dve.scalar_tensor_tensor(out=view, in0=src, scalar=vec[:, c, i:i + 1], in1=view,
                                                           op0=ALU.mult, op1=ALU.add)
                        ins.then_inc(conv_step.sem, 1)

            def multiplier_squared(b):
                for c in range(C):
                    square_done.wait(dve, b, c + 1)
                    decay_done.wait(dve, b, 2 * C)
                    dve.scalar_tensor_tensor(out=tnh[:, c, :], in0=mult[:, c, :], scalar=1.0, in1=tnh[:, c, :],
                                             op0=ALU.add, op1=ALU.mult).then_inc(multsq_done.sem, 1)

            def scan(b):
                resid_done.wait(dve, b, 0)
                for c in range(C):
                    square_done.wait(dve, b, c + 1)
                    dve.memset(a[:, c, :].rearrange("p (s t) -> p s t", s=SPB)[:, :, 0:1], 0.0)\
                        .then_inc(scan_step.sem, 1)
                    sqrt_done.wait(dve, b, c + 1)
                    gated_done.wait(dve, b, c + 1)
                    dve.tensor_tensor(h[:, c, :], gated[:, c, :], mult[:, c, :], ALU.mult).then_inc(scan_step.sem, 1)
                    scan_step.wait(dve, b, 4 * c + 2)
                    dve.tensor_tensor_scan(h[:, c, :], a[:, c, :], h[:, c, :], 0.0, ALU.mult, ALU.add)\
                        .then_inc(scan_step.sem, 1)
                    scan_step.wait(dve, b, 4 * c + 3)
                    xy_taken.wait(dve, b, C + c + 1)
                    dve.tensor_tensor(h[:, c, :], h[:, c, :], gelu_y[:, c, :], ALU.mult).then_inc(scan_step.sem, 1)

            def x1(b):
                for n in range(2):
                    resid_done.wait(dve, b, n + 1)
                    tiles = x_all[:, bass.ds(b * TPB + 2 * n, 2), :]
                    dve.tensor_tensor(tiles, pA[n][:].rearrange("p (t d) -> p t d", t=2), tiles, ALU.add)\
                        .then_inc(x1_done.sem, 1)

            def softmax_shift(b):
                def own(n, s):
                    return pS[n][SEQ * s:SEQ * s + SEQ, :].rearrange("p (t m s k) -> p t m s k", t=2, m=2, s=2)[:, :, :, s, :]
                for n in range(2):
                    score_done.wait(dve, b, n + 1)
                    for s in range(2):
                        dve.tensor_reduce(smax[SEQ * s:SEQ * s + SEQ, 2 * n:2 * n + 2], own(n, s), AX.XY, ALU.max)\
                            .then_inc(max_done.sem, 1)
                for n in range(2):
                    for s in range(2):
                        max_done.wait(dve, b, 2 * n + s + 1)
                        rows = slice(SEQ * s, SEQ * s + SEQ)
                        for u in range(2):
                            t = 2 * n + u
                            ins = dve.tensor_scalar(probs[rows, t, :, s, :], own(n, s)[:, u, :, :],
                                                    smax[rows, t:t + 1], None, ALU.subtract)
                        ins.then_inc(sub_done.sem, 1)

            def softmax_sum(b):
                exp_done.wait(dve, b, 2)
                dve.tensor_reduce(ssum[:], probs[:].rearrange("p t m s k -> p t (m s k)"), AX.X, ALU.add)\
                    .then_inc(sum_done.sem, 1)
                sum_done.wait(dve, b, 1)
                dve.reciprocal(sinv[:], ssum[:]).then_inc(sum_done.sem, 1)

            def x2(b):
                sum_done.wait(dve, b, 2)
                for t in range(TPB):
                    if t % 2 == 0:
                        pv_done.wait(dve, b, t // 2 + 1)
                    tile = x_all[:, bass.ds(b * TPB + t, 1), :].rearrange("p o d -> p (o d)")
                    dve.scalar_tensor_tensor(out=tile, in0=pS[t // 2][:, D * (t % 2):D * (t % 2) + D],
                                             scalar=sinv[:, t:t + 1], in1=tile, op0=ALU.mult, op1=ALU.add)\
                        .then_inc(x2_done.sem, 1)

            def router_out(b):
                router_done.wait(dve, b, 1)
                dve.tensor_copy(logits[:, bass.ds(b * TPB, TPB), :],
                                pB[0][:, 0:TPB * E].rearrange("p (t e) -> p t e", t=TPB)).then_inc(router_taken.sem, 1)

            steps = [0]

            def setup(ins):
                steps[0] += 1
                ins.then_inc(s_setup, 1)
                dve.wait_ge(s_setup, steps[0])

            dve.wait_ge(s_vec, 32)
            setup(dve.scalar_tensor_tensor(out=sp[:, 0, :], in0=vec[:, :, 7], scalar=-1.0, in1=vec[:, :, 7],
                                           op0=ALU.mult, op1=ALU.max))
            setup(dve.reciprocal(inv_temp[:], temp[:]))
            dve.wait_ge(s_sp_act, 1)
            setup(dve.tensor_scalar(sp[:, 2, :], sp[:, 1, :], 2.0, None, ALU.add))
            setup(dve.reciprocal(sp[:, 2, :], sp[:, 2, :]))
            setup(dve.tensor_tensor(sp[:, 3, :], sp[:, 1, :], sp[:, 2, :], ALU.mult))
            setup(dve.tensor_tensor(sp[:, 4, :], sp[:, 3, :], sp[:, 3, :], ALU.mult))
            setup(dve.memset(sp[:, 2, :], 0.0))
            for k in range(ATANH_TERMS, 0, -1):
                setup(dve.scalar_tensor_tensor(out=sp[:, 2, :], in0=sp[:, 2, :], scalar=1.0 / (2 * k + 1),
                                               in1=sp[:, 4, :], op0=ALU.add, op1=ALU.mult))
            setup(dve.scalar_tensor_tensor(out=sp[:, 2, :], in0=sp[:, 2, :], scalar=1.0, in1=sp[:, 3, :],
                                           op0=ALU.add, op1=ALU.mult))
            setup(dve.tensor_scalar(sp[:, 4, :], vec[:, :, 7], 0.0, 8.0, ALU.max, ALU.mult))
            setup(dve.scalar_tensor_tensor(out=decay[:], in0=sp[:, 2, :], scalar=16.0, in1=sp[:, 4, :],
                                           op0=ALU.mult, op1=ALU.add))
            setup(dve.tensor_scalar(neg_decay[:], decay[:], -1.0, None, ALU.mult))
            assert steps[0] == SETUP_STEPS

            dve.wait_ge(s_x0, 16)
            ln1(0)
            conv(0)
            multiplier_squared(0)
            scan(0)
            x1(0)
            ln2(0)
            dve.wait_ge(s_xrest, 16)
            with dve.Fori(1, NB) as i:
                ln1(i)
                conv(i)
                softmax_shift(i - 1)
                multiplier_squared(i)
                scan(i)
                softmax_sum(i - 1)
                x2(i - 1)
                x1(i)
                ln3(i - 1)
                ln2(i)
                router_out(i - 1)
            softmax_shift(NB - 1)
            softmax_sum(NB - 1)
            x2(NB - 1)
            ln3(NB - 1)
            router_out(NB - 1)

            route_n = [0]

            def route(ins):
                route_n[0] += 1
                ins.then_inc(s_route, 1)
                dve.wait_ge(s_route, route_n[0])

            def spread(v):
                return v.unsqueeze(2).to_broadcast([P, NT, E])

            dve.wait_ge(router_taken.sem, NB + 1)
            route(dve.tensor_scalar(inside, logits[:], inv_temp[:, 0:1], None, ALU.mult))
            assert route_n[0] == R_LOGIT
            dve.wait_ge(s_route_act, 1)
            route(dve.tensor_scalar(zone, inside, GOLDEN_CENTER, None, ALU.subtract))
            route(dve.scalar_tensor_tensor(out=dist, in0=zone, scalar=-1.0, in1=zone, op0=ALU.mult, op1=ALU.max))
            assert route_n[0] == R_DIST
            route(dve.tensor_scalar(zone, inside, GOLDEN_UPPER, None, ALU.is_le))
            route(dve.scalar_tensor_tensor(out=zone, in0=inside, scalar=GOLDEN_LOWER, in1=zone,
                                           op0=ALU.is_ge, op1=ALU.mult))
            dve.wait_ge(s_route_act, 3)
            route(dve.tensor_tensor(golden, golden, zone, ALU.mult))
            route(dve.tensor_reduce(gsum, golden, AX.X, ALU.add))
            route(dve.tensor_scalar(none_in, gsum, 1e-8, None, ALU.is_lt))
            fb_i = fallback.unsqueeze(3).to_broadcast([P, NT, E, E])
            fb_j = fallback.unsqueeze(2).to_broadcast([P, NT, E, E])
            route(dve.tensor_tensor(above, fb_j, fb_i, ALU.is_gt))
            route(dve.tensor_tensor(equal, fb_j, fb_i, ALU.is_equal))
            dve.wait_ge(s_const, 5)
            route(dve.tensor_tensor(equal.rearrange("p t i j -> p t (i j)"), equal.rearrange("p t i j -> p t (i j)"),
                                    earlier[:].unsqueeze(1).to_broadcast([P, NT, E * E]), ALU.mult))
            route(dve.tensor_tensor(above, above, equal, ALU.add))
            route(dve.tensor_reduce(rank, above, AX.X, ALU.add))
            route(dve.scalar_tensor_tensor(out=fallback, in0=rank, scalar=2.0, in1=fallback,
                                           op0=ALU.is_lt, op1=ALU.mult))
            route(dve.tensor_reduce(fsum, fallback, AX.X, ALU.add))
            route(dve.tensor_scalar(fsum, fsum, 1e-8, None, ALU.max))
            route(dve.reciprocal(fsum, fsum))
            route(dve.tensor_tensor(fsum, fsum, none_in, ALU.mult))
            route(dve.tensor_tensor(fallback, fallback, spread(fsum), ALU.mult))
            route(dve.tensor_scalar(none_in, none_in, -1.0, 1.0, ALU.mult, ALU.add))
            route(dve.tensor_tensor(golden, golden, spread(none_in), ALU.mult))
            route(dve.tensor_tensor(golden, golden, fallback, ALU.add))
            route(dve.tensor_reduce(gsum, golden, AX.X, ALU.add))
            route(dve.tensor_scalar(gsum, gsum, 1e-8, None, ALU.max))
            route(dve.reciprocal(gsum, gsum))
            route(dve.tensor_tensor(combine[:], golden, spread(gsum), ALU.mult))

            def gated_up(n, j):
                if j:
                    hlo_done.wait(dve, n - 1, 0)
                for f in range(C):
                    silu_done.wait(dve, n, f + 1)
                    gu_done.wait(dve, n, f + 1)
                    dve.tensor_tensor(h_raw[j % 2][:, f, :], up_bank(f)[:], silu_g[:, j % 2, f, :], ALU.mult)\
                        .then_inc(hraw_done.sem, 1)

            def accumulate(n, e, j):
                acc_done.wait(dve, n, 0)
                for t in range(TPB):
                    if t % 2 == 0:
                        down_done.wait(dve, n, t // 2 + 1)
                    at = TPB * (j % STEPS) + t
                    weight = combine[:, at, bass.ds(e, 1)]
                    dve.scalar_tensor_tensor(out=x_all[:, at, :], in0=down_bank(t // 2)[:, D * (t % 2):D * (t % 2) + D],
                                             scalar=weight, in1=x_all[:, at, :], op0=ALU.mult, op1=ALU.add)\
                        .then_inc(acc_done.sem, 1)

            gated_up(0, 0)
            with dve.Fori(0, E // 2 - 1) as pair:
                for j in range(2 * STEPS):
                    n = pair * 2 * STEPS + j
                    gated_up(n + 1, j + 1)
                    accumulate(n, pair * 2 + j // STEPS, j)
            for j in range(2 * STEPS):
                n = (E - 2) * STEPS + j
                if j < 2 * STEPS - 1:
                    gated_up(n + 1, j + 1)
                accumulate(n, E - 2 + j // STEPS, j)


def lay_rows(w):
    return w.reshape(2, 128, -1).transpose(1, 0, 2)


def kernel(**inputs):
    import numpy as np
    import concourse.bacc as bacc
    from concourse.bass_utils import run_bass_kernel_spmd

    v = {n: np.asarray(a) for n, a in inputs.items()}
    B, S, d = v["x"].shape
    tokens = B * S

    def block_diagonal(w):
        out = np.zeros((2, 8, 16, 8, 16), w.dtype)
        for n in range(8):
            out[:, n, :, n, :] = w.reshape(2, 8, 16, 16)[:, n]
        return out.reshape(2, 128, 128).transpose(1, 0, 2)

    def flat(*parts):
        return np.ascontiguousarray(np.concatenate([p.reshape(128, -1) for p in parts], axis=1))

    def channels(a):
        return a.reshape(2, 128).T.reshape(128, 2, 1)

    w_stage1 = flat(lay_rows(v["L0_attn_W_xy"].T), block_diagonal(v["L0_attn_ig_w"]),
                    block_diagonal(v["L0_attn_ag_w"]), lay_rows(v["L0_attn_W_resid"].T))
    w_stage2 = flat(lay_rows(v["L0_xattn_wq"].T), lay_rows(v["L0_xattn_wk"].T), lay_rows(v["L0_xattn_wo"].T),
                    lay_rows(v["L0_xattn_wv"]), lay_rows(v["L0_ffn_Wr"]))
    vecs = np.ascontiguousarray(np.concatenate(
        [channels(v["L0_attn_conv_w"][i]) for i in range(4)]
        + [channels(v[n]) for n in ("L0_attn_conv_b", "L0_attn_ig_b", "L0_attn_ag_b", "L0_attn_a_param")], axis=2))
    experts = np.stack([v["L0_ffn_Wg"], v["L0_ffn_Wu"], v["L0_ffn_Wd"]], axis=1)
    experts = experts.reshape(experts.shape[0], 3, 2, 128, 256).transpose(0, 3, 1, 2, 4)
    ctx_t = v["ctx_2048"].reshape(tokens // BLK, BLK, 2, 128).transpose(0, 3, 2, 1)
    arrays = {
        "x": np.ascontiguousarray(v["x"].reshape(tokens, d)),
        "ctx_t": np.ascontiguousarray(ctx_t),
        "w_stage1": w_stage1,
        "w_stage2": w_stage2,
        "channel_vecs": vecs,
        "w_experts": np.ascontiguousarray(experts).reshape(experts.shape[0], 128, -1),
        "temperature": np.ascontiguousarray(v["L0_ffn_temperature"]),
    }
    nc = bacc.Bacc("TRN2", target_bir_lowering=False, num_devices=1)
    args = [nc.dram_tensor(n, a.shape, mybir.dt.from_np(a.dtype), kind="ExternalInput").ap() for n, a in arrays.items()]
    out = nc.dram_tensor("out", (tokens, d), F32, kind="ExternalOutput").ap()
    decoder_kernel(nc, *args, out)
    result = run_bass_kernel_spmd(nc, [arrays], core_ids=[0])
    return result.results[0]["out"].reshape(B, S, d)
```

```python
from contextlib import ExitStack

import concourse.bass as bass
from concourse import mybir

ALU = mybir.AluOpType
ACT = mybir.ActivationFunctionType
AX = mybir.AxisListType
F32 = mybir.dt.float32
F32R = mybir.dt.float32r

P = 128
SEQ = 64
D = 256
C = D // P
BLK = 512
TPB = BLK // P
SPB = BLK // SEQ
CW = 4
PADDED = SEQ + CW - 1
SCALE = 1.0 / 16.0
EPS = 1e-5
GOLDEN_CENTER = 0.36787944117144233
GOLDEN_LOWER = 0.21231792754821915
GOLDEN_UPPER = 0.5
ATANH_TERMS = 9


class Tally:

    def __init__(self, sem, per_block, base=0):
        self.sem, self.per_block, self.base = sem, per_block, base

    def start(self, eng):
        eng.sem_inc(self.sem, self.base)

    def at(self, b, k):
        return b * self.per_block + (k + self.base)

    def before(self, b):
        return self.at(b, 0)


def decoder_kernel(nc, x, ctx_t, w_xy_d, w_qko_d, w_stage1, w_stage2, channel_vecs, w_experts, temperature, out):
    tokens = x.shape[0]
    NB = tokens // BLK
    NT = tokens // P
    E = w_experts.shape[0]
    WE = w_experts.shape[2]
    STEPS = NB
    PAIR = 2 * STEPS
    EARLY = 3

    x_tiles = x.rearrange("(t p) d -> p t d", p=P)
    out_tiles = out.rearrange("(t p) d -> p t d", p=P)

    with ExitStack() as stack:
        def sb(name, shape, dt=F32):
            return stack.enter_context(nc.sbuf_tensor(name, shape, dt))

        def sem(name):
            return stack.enter_context(nc.semaphore(name))

        def tally(name, per_block):
            return Tally(sem(name), per_block)

        def loop_tally(name, per_step):
            return Tally(sem(name), per_step, base=1)

        x_all = sb("x_all", [P, NT, D])
        x3t_hi = sb("x3t_hi", [P, C, tokens], F32R)
        x3t_lo = sb("x3t_lo", [P, C, tokens], F32R)
        combine = sb("combine", [P, NT, E])
        ident = sb("ident", [P, P])
        w_raw = sb("w_raw", [P, WE])
        w_hi = sb("w_hi", [P, 2, WE], F32R)
        w_lo = sb("w_lo", [P, 2, WE], F32R)
        w_xy_hi = sb("w_xy_hi", [P, C, 2 * D], F32R)
        w_xy_lo = sb("w_xy_lo", [P, C, 2 * D], F32R)
        w1 = sb("w1", [P, 2 * C * P + C * D])
        w_gates = w1[:, 0:2 * C * P].rearrange("p (g c n) -> p g c n", g=2, c=C)
        w_resid = w1[:, 2 * C * P:].rearrange("p (k n) -> p k n", k=C)
        w2 = sb("w2", [P, C * D + C * E])
        w_v = w2[:, 0:C * D].rearrange("p (k n) -> p k n", k=C)
        w_r = w2[:, C * D:].rearrange("p (k n) -> p k n", k=C)
        (w_q_hi, w_k_hi, w_o_hi), (w_q_lo, w_k_lo, w_o_lo) = (
            [w[:, 1, C * D * n:C * D * (n + 1)].rearrange("p (k n) -> p k n", k=C) for n in range(3)]
            for w in (w_hi, w_lo))
        w_vo_hi = sb("w_vo_hi", [P, C, D], F32R)
        w_vo_lo = sb("w_vo_lo", [P, C, D], F32R)
        vec = sb("vec", [P, C, 8])
        decay = sb("decay", [P, C])
        neg_decay = sb("neg_decay", [P, C])
        sp = sb("sp", [P, 5, C])
        temp = sb("temp", [P, 1])
        inv_temp = sb("inv_temp", [P, 1])
        exponent = sb("exponent", [P, TPB])
        earlier = sb("earlier", [P, E, E])
        stats = sb("stats", [P, 3, TPB, 6])
        mv = sb("mv", [P, 3, TPB, 2])
        var_eps = sb("var_eps", [P, 3, TPB])
        rstd = sb("rstd", [P, 3, TPB])
        xn = [sb(f"xn{n + 1}", [P, TPB, D]) for n in range(3)]
        h_hi = sb("h_hi", [P, 2, C, BLK], F32R)
        h_lo = sb("h_lo", [P, 2, C, BLK], F32R)
        x1t_hi, x1t_lo, x2t_hi, x2t_lo = h_hi[:, 0], h_lo[:, 0], h_hi[:, 1], h_lo[:, 1]
        xr_pad = sb("xr_pad", [P, C, SPB, PADDED])
        gelu_y = sb("gelu_y", [P, C, BLK])
        xc = sb("xc", [P, C, BLK])
        sig = sb("sig", [P, 2, C, BLK])
        gated = sb("gated", [P, C, BLK])
        a = sb("a", [P, C, BLK])
        tnh = sb("tnh", [P, C, BLK])
        mult = sb("mult", [P, C, BLK])
        h = sb("h", [P, C, BLK])
        ctxt = sb("ctxt", [P, C, BLK])
        ctxt_hi = sb("ctxt_hi", [P, C, BLK], F32R)
        ctxt_lo = sb("ctxt_lo", [P, C, BLK], F32R)
        qt = sb("qt", [P, C, BLK])
        knt = sb("knt", [P, C, BLK])
        v_ctx = sb("v_ctx", [P, TPB, D])
        v_new = sb("v_new", [P, TPB, D])
        smax = sb("smax", [P, TPB])
        ssum = sb("ssum", [P, TPB])
        sinv = sb("sinv", [P, TPB])
        probs = sb("probs", [P, TPB, 2, 2, SEQ])
        probs_t = sb("probs_t", [P, TPB, 2, P])
        x3t = sb("x3t", [P, C, BLK])
        inside, dist, zone, golden, fallback, rank = (sb(n, [P, TPB, E]) for n in (
            "inside", "dist", "zone", "golden", "fallback", "rank"))
        gsum, none_in, fsum = (sb(n, [P, TPB]) for n in ("gsum", "none_in", "fsum"))
        above, equal = (probs_t[:, n, :, :].rearrange("p m q -> p (m q)").rearrange("p (t i j) -> p t i j", t=TPB, i=E)
                        for n in range(2))
        silu_g = sig
        h_raw = [gated, a]

        banks = [stack.enter_context(nc.psum_tensor(f"bank{n}", [P, BLK], F32)) for n in range(8)]
        pT = banks[0:2]
        pA = banks[2:4]
        pB = banks[4:6]
        pS = banks[6:8]

        s_x0 = sem("x_block0_in")
        s_xrest = sem("x_rest_in")
        s_w1 = sem("w1_in")
        s_w2 = sem("w2_in")
        s_vec = sem("vec_in")
        s_out = sem("out_written")
        s_ctx = sem("ctx_in")
        s_ident = sem("ident_ready")
        s_const = sem("const_ready")
        s_sp_act = sem("softplus_act")
        s_setup = sem("dve_setup")
        s_wvo = sem("wvo_ready")
        s_wvo_hi = sem("wvo_hi")
        s_wvo_lo = sem("wvo_lo")
        s_wxy_in = sem("raw_w_xy_in")
        s_wxy_hi = sem("w_xy_hi")
        s_wxy_lo = sem("w_xy_lo")
        s_landed = sem("raw_weights_in")
        pool_passed = sem("pool_waits_passed")
        ln_stats = [tally(f"ln{n + 1}_stats", TPB + 2) for n in range(3)]
        ln_rstd = [tally(f"ln{n + 1}_rstd", 1) for n in range(3)]
        ln_done = [tally(f"ln{n + 1}_done", TPB) for n in range(3)]
        t_done = [tally(f"t{n + 1}_done", C) for n in range(3)]
        t_hi = [tally(f"t{n + 1}_hi", C) for n in range(3)]
        t_lo = [tally(f"t{n + 1}_lo", C) for n in range(2)]
        tp_done = tally("probs_transposed", 2)
        tp_taken = tally("probs_t_taken", 2)
        xr_done = tally("xr_done", C)
        xr_taken = tally("xr_taken", C)
        y_done = tally("y_done", C)
        y_taken = tally("y_taken", C)
        conv_step = tally("conv_step", C * CW)
        gate_done = tally("gate_done", 4)
        gate_taken = tally("gate_taken", 4)
        gated_done = tally("gated_done", C)
        decay_done = tally("decay_done", 2 * C)
        square_done = tally("square_done", C)
        multsq_done = tally("multsq_done", C)
        sqrt_done = tally("sqrt_done", C)
        scan_step = tally("scan_step", 4 * C)
        resid_done = tally("resid_done", 2)
        x1_done = tally("x1_done", 2)
        ctx_hi = tally("ctx_hi", C)
        ctx_lo = tally("ctx_lo", C)
        q_done = tally("q_done", C)
        q_taken = tally("q_taken", C)
        k_done = tally("k_done", C)
        k_taken = tally("k_taken", C)
        v_done = tally("v_done", 4)
        v_taken = tally("v_taken", 4)
        score_done = tally("score_done", 2)
        max_done = tally("max_done", 4)
        sub_done = tally("sub_done", 4)
        exp_done = tally("exp_done", 2)
        sum_done = tally("sum_done", 2)
        pv_done = tally("pv_done", 2)
        x2_done = tally("x2_done", TPB)
        router_done = tally("router_done", 1)
        route_step = tally("route_step", 26)
        route_act = tally("route_act", 3)
        split3 = tally("x3_split", 2 * C)
        gu_done = loop_tally("gate_up_done", C)
        silu_done = loop_tally("silu_done", C)
        hraw_done = loop_tally("h_done", C)
        hhi_done = loop_tally("h_hi_done", C)
        hlo_done = loop_tally("h_lo_done", C)
        down_done = loop_tally("down_done", 2)
        acc_done = loop_tally("acc_done", TPB)
        whi_done = loop_tally("w_hi_done", 1)
        wlo_done = loop_tally("w_lo_done", 1)
        QKO, EXPERT0 = 0, 1
        R_LOGIT, R_DIST = 1, 3
        SETUP_STEPS = 7 + ATANH_TERMS + 4

        def gu_banks(n, f):
            if isinstance(n, int) and n < EARLY:
                return banks[2], banks[3]
            return banks[2 * f], banks[2 * f + 1]

        def down_bank(half):
            return banks[4 + half]

        block = stack.enter_context(nc.Block())

        @block.sync
        def _(sp_eng):
            sp_eng.dma_start(x_all[:, 0:TPB, :], x_tiles[:, 0:TPB, :]).then_inc(s_x0, 16)
            sp_eng.dma_start(w_raw[:, 0:C * 2 * D], w_xy_d).then_inc(s_wxy_in, 16)
            sp_eng.dma_start(ctxt[:], ctx_t[0]).then_inc(s_ctx, 16)
            sp_eng.dma_start(x_all[:, TPB:, :], x_tiles[:, TPB:, :]).then_inc(s_xrest, 16)
            sp_eng.wait_ge(s_wxy_lo, 1)
            sp_eng.dma_start(w_raw[:], w_qko_d).then_inc(s_landed, 16)
            sp_eng.wait_ge(wlo_done.sem, wlo_done.before(EXPERT0))
            sp_eng.wait_ge(s_wvo, C)
            sp_eng.dma_start(w_raw[:], w_experts[0]).then_inc(s_landed, 16)
            for b in range(1, NB):
                if b > 0:
                    sp_eng.wait_ge(ctx_lo.sem, ctx_lo.before(b))
                if b > 0:
                    sp_eng.wait_ge(score_done.sem, score_done.before(b))
                sp_eng.dma_start(ctxt[:], ctx_t[b]).then_inc(s_ctx, 16)
            with sp_eng.Fori(1, E) as e:
                sp_eng.wait_ge(wlo_done.sem, wlo_done.before(EXPERT0 + e))
                sp_eng.dma_start(w_raw[:], w_experts[bass.ds(e, 1)].rearrange("o p n -> (o p) n"))\
                    .then_inc(s_landed, 16)
            for b in range(NB):
                sp_eng.wait_ge(acc_done.sem, acc_done.at((E - 1) * STEPS + b, TPB))
                sp_eng.dma_start(out_tiles[:, TPB * b:TPB * b + TPB, :],
                                 x_all[:, TPB * b:TPB * b + TPB, :]).then_inc(s_out, 16)
            sp_eng.wait_ge(s_out, 16 * NB)

        @block.gpsimd
        def _(pool):
            for t in (hlo_done, whi_done, wlo_done):
                t.start(pool)
            pool.memset(exponent[:], -0.5).then_inc(s_const, 1)
            pool.memset(ident[:], 0.0).then_inc(s_ident, 1)
            pool.wait_ge(s_ident, 1)
            pool.affine_select(out=ident[:], in_=ident[:], compare_op=ALU.not_equal, fill=1.0, base=0,
                               pattern=[[-1, P]], channel_multiplier=1).then_inc(s_ident, 1)

            def split_landed(landing, n, hi, lo):
                pool.wait_ge(s_landed, landing * 16 + 16)
                pool.sem_inc(pool_passed, 1)
                pool.tensor_copy(hi, w_raw[:, 0:n]).then_inc(whi_done.sem, 1)
                pool.wait_ge(whi_done.sem, whi_done.at(landing, 1))
                pool.tensor_tensor(lo, w_raw[:, 0:n], hi.bitcast(F32), ALU.subtract).then_inc(wlo_done.sem, 1)

            def split_expert(e, parity):
                split_landed(EXPERT0 + e, WE, w_hi[:, parity, :], w_lo[:, parity, :])

            def inverse_deviation(n, b):
                pool.wait_ge(ln_stats[n].sem, ln_stats[n].at(b, TPB + 2))
                pool.tensor_tensor(rstd[:, n, :], var_eps[:, n, :], exponent[:], ALU.pow).then_inc(ln_rstd[n].sem, 1)

            def input_gate(b):
                for c in range(C):
                    pool.wait_ge(conv_step.sem, conv_step.at(b, CW * (c + 1)))
                    pool.wait_ge(gate_taken.sem, gate_taken.at(b, 2 * c + 1))
                    if b > 0:
                        pool.wait_ge(scan_step.sem, scan_step.before(b))
                    pool.tensor_tensor(gated[:, c, :], xc[:, c, :], sig[:, 0, c, :], ALU.mult)\
                        .then_inc(gated_done.sem, 1)

            def split_ctx(b):
                pool.wait_ge(s_ctx, 16 * b + 16)
                if b > 0:
                    pool.wait_ge(v_done.sem, v_done.at(b - 1, 2))
                for c in range(C):
                    pool.tensor_copy(ctxt_hi[:, c, :], ctxt[:, c, :]).then_inc(ctx_hi.sem, 1)
                for c in range(C):
                    pool.wait_ge(ctx_hi.sem, ctx_hi.at(b, c + 1))
                    pool.tensor_tensor(ctxt_lo[:, c, :], ctxt[:, c, :], ctxt_hi[:, c, :].bitcast(F32),
                                       ALU.subtract).then_inc(ctx_lo.sem, 1)

            def split_x3(b):
                cols = slice(BLK * b, BLK * b + BLK)
                for c in range(C):
                    pool.wait_ge(t_hi[2].sem, t_hi[2].at(b, c + 1))
                    pool.tensor_copy(x3t_hi[:, c, cols], x3t[:, c, :]).then_inc(split3.sem, 1)
                for c in range(C):
                    pool.wait_ge(split3.sem, split3.at(b, c + 1))
                    pool.tensor_tensor(x3t_lo[:, c, cols], x3t[:, c, :], x3t_hi[:, c, cols].bitcast(F32),
                                       ALU.subtract).then_inc(split3.sem, 1)

            def split_h(n, parity):
                for f in range(C):
                    pool.wait_ge(hraw_done.sem, hraw_done.at(n, f + 1))
                    pool.wait_ge(hhi_done.sem, hhi_done.at(n, f + 1))
                    pool.tensor_tensor(h_lo[:, parity, f, :], h_raw[parity][:, f, :],
                                       h_hi[:, parity, f, :].bitcast(F32), ALU.subtract).then_inc(hlo_done.sem, 1)

            def next_expert(e, parity):
                pool.wait_ge(down_done.sem, down_done.at((e - 1) * STEPS - 1, 2))
                split_expert(e, parity)

            pool.memset(xr_pad[:], 0.0).then_inc(s_const, 1)
            inverse_deviation(0, 0)
            pool.memset(earlier[:], 1.0).then_inc(s_const, 1)
            pool.wait_ge(s_const, 3)
            pool.affine_select(out=earlier[:], in_=earlier[:], compare_op=ALU.is_gt, fill=0.0, base=0,
                               pattern=[[1, E], [-1, E]], channel_multiplier=0).then_inc(s_const, 1)
            pool.memset(probs[:], 0.0).then_inc(s_const, 1)
            split_landed(QKO, WE, w_hi[:, 1, :], w_lo[:, 1, :])
            for i in range(NB + 1):
                if i == 0:
                    inverse_deviation(0, 1)
                if i < NB:
                    input_gate(i)
                if 0 < i < NB - 1:
                    inverse_deviation(0, i + 1)
                if i == 1:
                    split_expert(0, 0)
                if i >= 2:
                    split_x3(i - 2)
                if i < NB:
                    inverse_deviation(1, i)
                    split_ctx(i)
                if i == NB:
                    pool.wait_ge(q_done.sem, q_done.at(NB - 1, C))
                    pool.wait_ge(k_done.sem, k_done.at(NB - 1, C))
                    pool.wait_ge(v_done.sem, v_done.at(NB - 1, 2))
                    split_expert(1, 1)
                    split_h(0, 0)
                if i >= 1:
                    inverse_deviation(2, i - 1)
            split_h(1, 1)
            split_x3(NB - 1)
            split_h(2, 0)
            with pool.Fori(0, E // 2 - 1) as pair:
                for j in range(EARLY, EARLY + PAIR):
                    split_h(pair * PAIR + j, j % 2)
                    if j % STEPS == 0:
                        next_expert(pair * 2 + 1 + j // STEPS, (j // STEPS + 1) % 2)
            for n in range((E - 2) * STEPS + EARLY, E * STEPS):
                split_h(n, n % 2)

        @block.scalar
        def _(act):
            for t in (silu_done, hhi_done):
                t.start(act)
            act.dma_start(vec[:], channel_vecs).then_inc(s_vec, 16)
            act.dma_start(temp[:], temperature.partition_broadcast(P)).then_inc(s_vec, 16)
            act.dma_start(w1[:], w_stage1).then_inc(s_w1, 16)
            act.dma_start(w2[:], w_stage2).then_inc(s_w2, 16)
            act.wait_ge(s_setup, 1)
            act.activation(sp[:, 1, :], sp[:, 0, :], ACT.Exp, scale=-1.0).then_inc(s_sp_act, 1)
            act.wait_ge(s_wxy_in, 16)
            act.activation(w_xy_hi[:].rearrange("p k n -> p (k n)"), w_raw[:, 0:C * 2 * D], ACT.Copy).then_inc(s_wxy_hi, 1)

            def copy_out(b, psum, dst, ready, k, taken):
                act.wait_ge(ready.sem, ready.at(b, k + 1))
                act.activation(dst, psum, ACT.Copy).then_inc(taken.sem, 1)

            def take_t(n, b, dst):
                for c in range(C):
                    copy_out(b, pT[c][:], dst[:, c, :], t_done[n], c, t_hi[n])

            def take_xr(b):
                act.wait_ge(s_const, 2)
                if b > 0:
                    act.wait_ge(conv_step.sem, conv_step.before(b))
                for c in range(C):
                    copy_out(b, pA[c][:].rearrange("p (s t) -> p s t", s=SPB), xr_pad[:, c, :, CW - 1:PADDED],
                             xr_done, c, xr_taken)

            def gelus(b):
                if b > 0:
                    act.wait_ge(scan_step.sem, scan_step.before(b))
                for c in range(C):
                    act.wait_ge(y_done.sem, y_done.at(b, c + 1))
                    act.activation(gelu_y[:, c, :], pA[c][:], ACT.Gelu).then_inc(y_taken.sem, 1)

            def sigmoids(b):
                if b > 0:
                    act.wait_ge(gated_done.sem, gated_done.before(b))
                for c in range(C):
                    for g in range(2):
                        act.wait_ge(gate_done.sem, gate_done.at(b, 2 * c + g + 1))
                        act.activation(sig[:, g, c, :], pA[g][:], ACT.Sigmoid,
                                       bias=vec[:, c, 5 + g:6 + g]).then_inc(gate_taken.sem, 1)

            def decays(b):
                act.wait_ge(s_setup, SETUP_STEPS)
                if b > 0:
                    act.wait_ge(scan_step.sem, scan_step.before(b))
                act.wait_ge(gate_taken.sem, gate_taken.at(b, 4))
                for c in range(C):
                    act.activation(a[:, c, :], sig[:, 1, c, :], ACT.Exp,
                                   scale=neg_decay[:, c:c + 1]).then_inc(decay_done.sem, 1)
                for c in range(C):
                    act.wait_ge(decay_done.sem, decay_done.at(b, c + 1))
                    act.activation(mult[:, c, :], a[:, c, :], ACT.Square).then_inc(square_done.sem, 1)

            def tanhs(b):
                for c in range(C):
                    act.activation(tnh[:, c, :], sig[:, 1, c, :], ACT.Tanh,
                                   scale=decay[:, c:c + 1]).then_inc(decay_done.sem, 1)

            def roots(b):
                for c in range(C):
                    act.wait_ge(multsq_done.sem, multsq_done.at(b, c + 1))
                    act.activation(mult[:, c, :], tnh[:, c, :], ACT.Sqrt).then_inc(sqrt_done.sem, 1)

            def take_v(b, n):
                copy_out(b, pB[n % 2][:].rearrange("p (t d) -> p t d", t=2),
                         (v_ctx, v_new)[n // 2][:, 2 * (n % 2):2 * (n % 2) + 2, :], v_done, n, v_taken)

            def exponentials(b):
                for s in range(2):
                    act.wait_ge(sub_done.sem, sub_done.at(b, 4))
                    part = probs[SEQ * s:SEQ * s + SEQ, :, :, s, :]
                    act.activation(part, part, ACT.Exp, scale=SCALE).then_inc(exp_done.sem, 1)

            def take_tp(b):
                if b >= 2:
                    act.wait_ge(route_step.sem, route_step.before(b - 1))
                for n in range(2):
                    copy_out(b, pT[n][:].rearrange("p (t k q) -> p t k q", t=2, k=2),
                             probs_t[:, 2 * n:2 * n + 2, :, :], tp_done, n, tp_taken)

            def route_sigmoid(b):
                act.wait_ge(route_step.sem, route_step.at(b, R_LOGIT))
                act.activation(inside[:], inside[:], ACT.Sigmoid).then_inc(route_act.sem, 1)

            def route_exponentials(b):
                act.wait_ge(route_step.sem, route_step.at(b, R_DIST))
                act.activation(golden[:], dist[:], ACT.Exp, scale=-10.0).then_inc(route_act.sem, 1)
                act.activation(fallback[:], dist[:], ACT.Exp, scale=-1.0 / 0.3).then_inc(route_act.sem, 1)

            def silu(n, f, parity):
                act.wait_ge(gu_done.sem, gu_done.at(n, f + 1))
                act.activation(silu_g[:, parity, f, :], gu_banks(n, f)[0][:], ACT.Silu).then_inc(silu_done.sem, 1)

            def round_h(n, parity):
                for f in range(C):
                    act.wait_ge(hraw_done.sem, hraw_done.at(n, f + 1))
                    act.activation(h_hi[:, parity, f, :], h_raw[parity][:, f, :], ACT.Copy).then_inc(hhi_done.sem, 1)

            take_t(0, 0, x1t_hi)
            take_xr(0)
            for i in range(NB + 1):
                if i < NB:
                    sigmoids(i)
                if i == 0:
                    for k in range(C):
                        act.wait_ge(s_wvo, k + 1)
                        act.activation(w_vo_hi[:, k, :], pS[k][:, 0:D], ACT.Copy).then_inc(s_wvo_hi, 1)
                if i >= 1:
                    take_t(1, i - 1, x2t_hi)
                if i < NB:
                    decays(i)
                    tanhs(i)
                else:
                    silu(0, 0, 0)
                if i == 0:
                    take_t(0, 1, x1t_hi)
                if i >= 2:
                    if i > 2:
                        act.wait_ge(split3.sem, split3.before(i - 2))
                    take_t(2, i - 2, x3t)
                if i < NB:
                    roots(i)
                    gelus(i)
                if i >= 1:
                    for n in range(C):
                        copy_out(i - 1, pB[n][:], qt[:, n, :], q_done, n, q_taken)
                if i == NB:
                    route_sigmoid(NB - 2)
                    route_exponentials(NB - 2)
                if 0 < i < NB - 1:
                    take_t(0, i + 1, x1t_hi)
                if i >= 1:
                    for n in range(C):
                        copy_out(i - 1, pS[n][:], knt[:, n, :], k_done, n, k_taken)
                    take_v(i - 1, 0)
                    take_v(i - 1, 1)
                if 2 <= i < NB:
                    route_sigmoid(i - 2)
                if i < NB - 1:
                    take_xr(i + 1)
                if i >= 1:
                    exponentials(i - 1)
                if 2 <= i < NB:
                    route_exponentials(i - 2)
                if i == NB:
                    silu(0, 1, 0)
                if i >= 1:
                    take_v(i - 1, 2)
                    take_tp(i - 1)
                    take_v(i - 1, 3)
            round_h(0, 0)
            silu(1, 0, 1)
            silu(1, 1, 1)
            round_h(1, 1)
            act.wait_ge(split3.sem, split3.before(NB - 1))
            take_t(2, NB - 1, x3t)
            silu(2, 0, 0)
            silu(2, 1, 0)
            round_h(2, 0)
            route_sigmoid(NB - 1)
            route_exponentials(NB - 1)
            with act.Fori(0, E // 2 - 1) as pair:
                for j in range(EARLY, EARLY + PAIR):
                    for f in range(C):
                        silu(pair * PAIR + j, f, j % 2)
                    round_h(pair * PAIR + j, j % 2)
            for n in range((E - 2) * STEPS + EARLY, E * STEPS):
                for f in range(C):
                    silu(n, f, n % 2)
                round_h(n, n % 2)

        @block.tensor
        def _(pe):
            for t in (gu_done, down_done):
                t.start(pe)

            def product(dst, lhs, rhs, done=None):
                for k in range(C):
                    last = pe.matmul(dst, lhs(k), rhs(k), start=(k == 0), stop=(k == C - 1))
                if done is not None:
                    last.then_inc(done.sem, 1)

            def split_product(dst, lhs_hi, lhs_lo, rhs_hi, rhs_lo, done=None):
                n = 0
                for k in range(C):
                    for p, q in ((lhs_hi, rhs_hi), (lhs_hi, rhs_lo), (lhs_lo, rhs_hi)):
                        last = pe.matmul(dst, p(k), q(k), start=(n == 0), stop=(n == 3 * C - 1))
                        n += 1
                if done is not None:
                    last.then_inc(done.sem, 1)

            def transposes(n, b):
                for c in range(C):
                    for t in range(TPB):
                        if c == 0:
                            pe.wait_ge(ln_done[n].sem, ln_done[n].at(b, t + 1))
                        last = pe.transpose(pT[c][:, P * t:P * t + P], xn[n][:, t, P * c:P * c + P], ident[:])
                    last.then_inc(t_done[n].sem, 1)

            def xr(b):
                pe.wait_ge(t_lo[0].sem, t_lo[0].at(b, C))
                for n in range(C):
                    if b > 0:
                        pe.wait_ge(y_taken.sem, y_taken.at(b - 1, n + 1))
                    cols = slice(P * n, P * n + P)
                    split_product(pA[n][:], lambda k: w_xy_hi[:, k, cols], lambda k: w_xy_lo[:, k, cols],
                                  lambda k: x1t_hi[:, k, :], lambda k: x1t_lo[:, k, :], xr_done)

            def y(b):
                for n in range(C):
                    pe.wait_ge(gate_taken.sem, gate_taken.at(b, C + n + 1))
                    cols = slice(D + P * n, D + P * n + P)
                    split_product(pA[n][:], lambda k: w_xy_hi[:, k, cols], lambda k: w_xy_lo[:, k, cols],
                                  lambda k: x1t_hi[:, k, :], lambda k: x1t_lo[:, k, :], y_done)

            def gates(b, c):
                pe.wait_ge(conv_step.sem, conv_step.at(b, CW * (c + 1)))
                for g in range(2):
                    if c > 0:
                        pe.wait_ge(gate_taken.sem, gate_taken.at(b, g + 1))
                    elif b > 0:
                        pe.wait_ge(x1_done.sem, x1_done.at(b - 1, g + 1))
                    else:
                        pe.wait_ge(xr_taken.sem, xr_taken.at(b, g + 1))
                    pe.matmul(pA[g][:], w_gates[:, g, c, :], xc[:, c, :], start=True, stop=True)\
                        .then_inc(gate_done.sem, 1)

            def resid(b):
                pe.wait_ge(scan_step.sem, scan_step.at(b, 4 * C))
                for t in range(TPB):
                    if b < NB - 1:
                        pe.wait_ge(xr_taken.sem, xr_taken.at(b + 1, t // 2 + 1))
                    else:
                        pe.wait_ge(y_taken.sem, y_taken.at(b, t // 2 + 1))
                    dst = pA[t // 2][:, D * (t % 2):D * (t % 2) + D]
                    product(dst, lambda k: h[:, k, P * t:P * t + P], lambda k: w_resid[:, k, :],
                            resid_done if t % 2 else None)

            def queries(b):
                pe.wait_ge(t_lo[1].sem, t_lo[1].at(b, C))
                if b > 0:
                    pe.wait_ge(v_taken.sem, v_taken.before(b))
                for n in range(C):
                    cols = slice(P * n, P * n + P)
                    split_product(pB[n][:], lambda k: w_q_hi[:, k, cols], lambda k: w_q_lo[:, k, cols],
                                  lambda k: x2t_hi[:, k, :], lambda k: x2t_lo[:, k, :], q_done)

            def keys(b):
                if b > 0:
                    pe.wait_ge(x2_done.sem, x2_done.before(b))
                    pe.wait_ge(route_step.sem, route_step.at(b - 1, R_LOGIT))
                for n in range(C):
                    cols = slice(P * n, P * n + P)
                    split_product(pS[n][:], lambda k: w_k_hi[:, k, cols], lambda k: w_k_lo[:, k, cols],
                                  lambda k: x2t_hi[:, k, :], lambda k: x2t_lo[:, k, :], k_done)

            def values(b, n):
                if n < 2:
                    pe.wait_ge(ctx_lo.sem, ctx_lo.at(b, C))
                    pe.wait_ge(q_taken.sem, q_taken.at(b, n + 1))
                    hi, lo, w, wl = ctxt_hi, ctxt_lo, w_o_hi, w_o_lo
                else:
                    pe.wait_ge(v_taken.sem, v_taken.at(b, n - 1))
                    hi, lo, w, wl = x2t_hi, x2t_lo, w_vo_hi, w_vo_lo
                for u in range(2):
                    t = 2 * (n % 2) + u
                    tile = slice(P * t, P * t + P)
                    split_product(pB[n % 2][:, D * u:D * u + D], lambda k: hi[:, k, tile], lambda k: lo[:, k, tile],
                                  lambda k: w[:, k, :], lambda k: wl[:, k, :], v_done if u else None)

            def scores(b):
                pe.wait_ge(q_taken.sem, q_taken.at(b, C))
                pe.wait_ge(k_taken.sem, k_taken.at(b, C))
                for t in range(TPB):
                    pair = slice(P * t, P * t + P)
                    for m, key in enumerate((ctxt, knt)):
                        at = D * (t % 2) + P * m
                        for k in range(C):
                            last = pe.matmul(pS[t // 2][:, at:at + P], qt[:, k, pair], key[:, k, pair],
                                             start=(k == 0), stop=(k == C - 1))
                    if t % 2:
                        last.then_inc(score_done.sem, 1)

            def probs_transpose(b):
                pe.wait_ge(exp_done.sem, exp_done.at(b, 2))
                for t in range(TPB):
                    for m in range(2):
                        at = D * (t % 2) + P * m
                        last = pe.transpose(pT[t // 2][:, at:at + P],
                                            probs[:, t, m, :, :].rearrange("p s k -> p (s k)"), ident[:])
                    if t % 2:
                        last.then_inc(tp_done.sem, 1)

            def attend(b):
                pe.wait_ge(sub_done.sem, sub_done.at(b, 4))
                pe.wait_ge(v_taken.sem, v_taken.at(b, 4))
                for t in range(TPB):
                    pe.wait_ge(tp_taken.sem, tp_taken.at(b, t // 2 + 1))
                    dst = pS[t // 2][:, D * (t % 2):D * (t % 2) + D]
                    for m, v in enumerate((v_ctx, v_new)):
                        last = pe.matmul(dst, probs_t[:, t, m, :], v[:, t, :], start=(m == 0), stop=(m == 1))
                    if t % 2:
                        last.then_inc(pv_done.sem, 1)

            def router(b):
                pe.wait_ge(t_hi[2].sem, t_hi[2].at(b, C))
                pe.wait_ge(x2_done.sem, x2_done.at(b, TPB))
                for t in range(TPB):
                    product(pS[0][:, E * t:E * t + E], lambda k: x3t[:, k, P * t:P * t + P], lambda k: w_r[:, k, :],
                            router_done if t == TPB - 1 else None)

            def gate_up(n, j, f):
                par, cols = (j // STEPS) % 2, slice(BLK * (j % STEPS), BLK * (j % STEPS) + BLK)
                for which in range(2):
                    def at(k):
                        start = (which * C + k) * D + P * f
                        return slice(start, start + P)
                    split_product(gu_banks(n, f)[which][:], lambda k: w_hi[:, par, at(k)], lambda k: w_lo[:, par, at(k)],
                                  lambda k: x3t_hi[:, k, cols], lambda k: x3t_lo[:, k, cols],
                                  gu_done if which else None)

            def gate_ups(n, j):
                for f in range(C):
                    pe.wait_ge(hraw_done.sem, hraw_done.at(n - 1, f + 1))
                    gate_up(n, j, f)

            def down(n, j):
                par = (j // STEPS) % 2
                pe.wait_ge(acc_done.sem, acc_done.before(n))
                pe.wait_ge(hlo_done.sem, hlo_done.at(n, C))
                for t in range(TPB):
                    def rows(f):
                        start = (2 * C + f) * D
                        return slice(start, start + D)
                    tile = slice(P * t, P * t + P)
                    split_product(down_bank(t // 2)[:, D * (t % 2):D * (t % 2) + D],
                                  lambda f: h_hi[:, j % 2, f, tile], lambda f: h_lo[:, j % 2, f, tile],
                                  lambda f: w_hi[:, par, rows(f)], lambda f: w_lo[:, par, rows(f)],
                                  down_done if t % 2 else None)

            pe.wait_ge(s_ident, 2)
            transposes(0, 0)
            pe.wait_ge(s_wxy_lo, 1)
            xr(0)
            pe.wait_ge(s_w2, 16)
            pe.wait_ge(s_landed, 16)
            for k in range(C):
                for j in range(C):
                    last = pe.matmul(pS[k][:, 0:D], w_v[:, j, P * k:P * k + P],
                                     w_raw[:, (2 * C + j) * D:(2 * C + j + 1) * D],
                                     start=(j == 0), stop=(j == C - 1))
                last.then_inc(s_wvo, 1)
            pe.wait_ge(s_w1, 16)
            gates(0, 0)
            for i in range(NB + 1):
                if i >= 1:
                    transposes(1, i - 1)
                if i < NB:
                    gates(i, 1)
                if i < NB:
                    y(i)
                if i >= 2:
                    pe.wait_ge(t_lo[1].sem, t_lo[1].at(i - 1, C))
                    transposes(2, i - 2)
                if i >= 1:
                    if i == 1:
                        pe.wait_ge(wlo_done.sem, wlo_done.at(QKO, 1))
                        pe.wait_ge(s_wvo_lo, C)
                    queries(i - 1)
                if i >= 2:
                    router(i - 2)
                if i < NB - 1:
                    transposes(0, i + 1)
                if i >= 1:
                    keys(i - 1)
                    values(i - 1, 0)
                    values(i - 1, 1)
                    scores(i - 1)
                if i < NB - 1:
                    xr(i + 1)
                if i < NB:
                    resid(i)
                else:
                    pe.wait_ge(hraw_done.sem, hraw_done.at(0, 1))
                    gate_up(0, 0, 1)
                if i >= 1:
                    values(i - 1, 2)
                    probs_transpose(i - 1)
                    values(i - 1, 3)
                if i < NB - 1:
                    gates(i + 1, 0)
                elif i == NB - 1:
                    pe.wait_ge(wlo_done.sem, wlo_done.at(EXPERT0, 1))
                    pe.wait_ge(x1_done.sem, x1_done.at(NB - 1, 2))
                    gate_up(0, 0, 0)
                if i >= 1:
                    attend(i - 1)
            for n in range(1, EARLY):
                pe.wait_ge(hraw_done.sem, hraw_done.at(n - 1, C))
                gate_up(n, n, 0)
                down(n - 1, n - 1)
                pe.wait_ge(hraw_done.sem, hraw_done.at(n, 1))
                gate_up(n, n, 1)
                if n == 1:
                    transposes(2, NB - 1)
                    router(NB - 1)
            pe.wait_ge(split3.sem, split3.at(NB - 1, 2 * C))
            with pe.Fori(0, E // 2 - 1) as pair:
                for j in range(EARLY, EARLY + PAIR):
                    if j % STEPS == 0:
                        pe.wait_ge(wlo_done.sem, wlo_done.at(pair * 2 + (EXPERT0 + j // STEPS), 1))
                    gate_ups(pair * PAIR + j, j)
                    down(pair * PAIR + (j - 1), j - 1)
            for n in range((E - 2) * STEPS + EARLY, E * STEPS + 1):
                if n < E * STEPS:
                    if n % STEPS == 0:
                        pe.wait_ge(wlo_done.sem, wlo_done.at(EXPERT0 + n // STEPS, 1))
                    gate_ups(n, n)
                down(n - 1, n - 1)

        @block.vector
        def _(dve):
            for t in (hraw_done, acc_done):
                t.start(dve)

            def layernorm(n, b):
                if b > 0:
                    dve.wait_ge(t_done[n].sem, t_done[n].before(b))
                if n:
                    dve.wait_ge((x1_done, x2_done)[n - 1].sem, (x1_done, x2_done)[n - 1].at(b, (2, TPB)[n - 1]))
                for t in range(TPB):
                    dve.bn_stats(stats[:, n, t, :], x_all[:, TPB * b + t, :]).then_inc(ln_stats[n].sem, 1)
                for t in range(TPB):
                    dve.wait_ge(ln_stats[n].sem, ln_stats[n].at(b, t + 1))
                    ins = dve.bn_aggr(mv[:, n, t, :], stats[:, n, t, :])
                ins.then_inc(ln_stats[n].sem, 1)
                dve.wait_ge(ln_stats[n].sem, ln_stats[n].at(b, TPB + 1))
                dve.tensor_scalar(var_eps[:, n, :], mv[:, n, :, 1], EPS, None, ALU.add).then_inc(ln_stats[n].sem, 1)

            def normalize(n, b):
                dve.wait_ge(ln_rstd[n].sem, ln_rstd[n].at(b, 1))
                for t in range(TPB):
                    dve.tensor_scalar(xn[n][:, t, :], x_all[:, TPB * b + t, :], mv[:, n, t, 0:1], rstd[:, n, t:t + 1],
                                      ALU.subtract, ALU.mult).then_inc(ln_done[n].sem, 1)

            def rest_of_t(n, b, hi, lo):
                for c in range(C):
                    dve.wait_ge(t_hi[n].sem, t_hi[n].at(b, c + 1))
                    dve.tensor_tensor(lo[:, c, :], pT[c][:], hi[:, c, :].bitcast(F32), ALU.subtract)\
                        .then_inc(t_lo[n].sem, 1)

            def conv(b):
                if b > 0:
                    dve.wait_ge(gate_done.sem, gate_done.before(b))
                if b > 0:
                    dve.wait_ge(gated_done.sem, gated_done.before(b))
                for c in range(C):
                    dve.wait_ge(xr_taken.sem, xr_taken.at(b, c + 1))
                    view = xc[:, c, :].rearrange("p (s t) -> p s t", s=SPB)
                    for i in range(CW):
                        src = xr_pad[:, c, :, i:i + SEQ]
                        if i == 0:
                            ins = dve.tensor_scalar(view, src, vec[:, c, 0:1], vec[:, c, 4:5], ALU.mult, ALU.add)
                        else:
                            dve.wait_ge(conv_step.sem, conv_step.at(b, CW * c + i))
                            ins = dve.scalar_tensor_tensor(out=view, in0=src, scalar=vec[:, c, i:i + 1], in1=view,
                                                           op0=ALU.mult, op1=ALU.add)
                        ins.then_inc(conv_step.sem, 1)

            def multiplier_squared(b):
                for c in range(C):
                    dve.wait_ge(square_done.sem, square_done.at(b, c + 1))
                    dve.wait_ge(decay_done.sem, decay_done.at(b, C + c + 1))
                    dve.scalar_tensor_tensor(out=tnh[:, c, :], in0=mult[:, c, :], scalar=1.0, in1=tnh[:, c, :],
                                             op0=ALU.add, op1=ALU.mult).then_inc(multsq_done.sem, 1)

            def scan(b):
                if b > 0:
                    dve.wait_ge(resid_done.sem, resid_done.before(b))
                for c in range(C):
                    dve.wait_ge(square_done.sem, square_done.at(b, c + 1))
                    dve.memset(a[:, c, :].rearrange("p (s t) -> p s t", s=SPB)[:, :, 0:1], 0.0)\
                        .then_inc(scan_step.sem, 1)
                    dve.wait_ge(sqrt_done.sem, sqrt_done.at(b, c + 1))
                    dve.wait_ge(gated_done.sem, gated_done.at(b, c + 1))
                    dve.tensor_tensor(h[:, c, :], gated[:, c, :], mult[:, c, :], ALU.mult).then_inc(scan_step.sem, 1)
                    dve.wait_ge(scan_step.sem, scan_step.at(b, 4 * c + 2))
                    dve.tensor_tensor_scan(h[:, c, :], a[:, c, :], h[:, c, :], 0.0, ALU.mult, ALU.add)\
                        .then_inc(scan_step.sem, 1)
                    dve.wait_ge(scan_step.sem, scan_step.at(b, 4 * c + 3))
                    dve.wait_ge(y_taken.sem, y_taken.at(b, c + 1))
                    dve.tensor_tensor(h[:, c, :], h[:, c, :], gelu_y[:, c, :], ALU.mult).then_inc(scan_step.sem, 1)

            def x1(b):
                for n in range(2):
                    dve.wait_ge(resid_done.sem, resid_done.at(b, n + 1))
                    tiles = x_all[:, TPB * b + 2 * n:TPB * b + 2 * n + 2, :]
                    dve.tensor_tensor(tiles, pA[n][:].rearrange("p (t d) -> p t d", t=2), tiles, ALU.add)\
                        .then_inc(x1_done.sem, 1)

            def softmax_shift(b):
                def own(n, s):
                    return pS[n][SEQ * s:SEQ * s + SEQ, :].rearrange("p (t m s k) -> p t m s k", t=2, m=2, s=2)[:, :, :, s, :]
                for n in range(2):
                    dve.wait_ge(score_done.sem, score_done.at(b, n + 1))
                    for s in range(2):
                        dve.tensor_reduce(smax[SEQ * s:SEQ * s + SEQ, 2 * n:2 * n + 2], own(n, s), AX.XY, ALU.max)\
                            .then_inc(max_done.sem, 1)
                for n in range(2):
                    for s in range(2):
                        dve.wait_ge(max_done.sem, max_done.at(b, 2 * n + s + 1))
                        rows = slice(SEQ * s, SEQ * s + SEQ)
                        for u in range(2):
                            t = 2 * n + u
                            ins = dve.tensor_scalar(probs[rows, t, :, s, :], own(n, s)[:, u, :, :],
                                                    smax[rows, t:t + 1], None, ALU.subtract)
                        ins.then_inc(sub_done.sem, 1)

            def softmax_sum(b):
                dve.wait_ge(exp_done.sem, exp_done.at(b, 2))
                dve.tensor_reduce(ssum[:], probs[:].rearrange("p t m s k -> p t (m s k)"), AX.X, ALU.add)\
                    .then_inc(sum_done.sem, 1)
                dve.wait_ge(sum_done.sem, sum_done.at(b, 1))
                dve.reciprocal(sinv[:], ssum[:]).then_inc(sum_done.sem, 1)

            def x2(b):
                dve.wait_ge(sum_done.sem, sum_done.at(b, 2))
                for t in range(TPB):
                    if t % 2 == 0:
                        dve.wait_ge(pv_done.sem, pv_done.at(b, t // 2 + 1))
                    tile = x_all[:, TPB * b + t, :]
                    dve.scalar_tensor_tensor(out=tile, in0=pS[t // 2][:, D * (t % 2):D * (t % 2) + D],
                                             scalar=sinv[:, t:t + 1], in1=tile, op0=ALU.mult, op1=ALU.add)\
                        .then_inc(x2_done.sem, 1)

            def route_logits(b):
                dve.wait_ge(router_done.sem, router_done.at(b, 1))
                dve.tensor_scalar(inside[:], pS[0][:, 0:TPB * E].rearrange("p (t e) -> p t e", t=TPB),
                                  inv_temp[:, 0:1], None, ALU.mult).then_inc(route_step.sem, 1)

            def route_distance(b):
                dve.wait_ge(route_act.sem, route_act.at(b, 1))
                dve.tensor_scalar(zone[:], inside[:], GOLDEN_CENTER, None, ALU.subtract).then_inc(route_step.sem, 1)
                dve.wait_ge(route_step.sem, route_step.at(b, 2))
                dve.scalar_tensor_tensor(out=dist[:], in0=zone[:], scalar=-1.0, in1=zone[:], op0=ALU.mult,
                                         op1=ALU.max).then_inc(route_step.sem, 1)

            def route_weights(b):
                done = [R_DIST]

                def step(ins):
                    done[0] += 1
                    ins.then_inc(route_step.sem, 1)
                    dve.wait_ge(route_step.sem, route_step.at(b, done[0]))

                def spread(v):
                    return v[:].unsqueeze(2).to_broadcast([P, TPB, E])

                dve.wait_ge(route_step.sem, route_step.at(b, R_DIST))
                step(dve.tensor_scalar(zone[:], inside[:], GOLDEN_UPPER, None, ALU.is_le))
                step(dve.scalar_tensor_tensor(out=zone[:], in0=inside[:], scalar=GOLDEN_LOWER, in1=zone[:],
                                              op0=ALU.is_ge, op1=ALU.mult))
                dve.wait_ge(route_act.sem, route_act.at(b, 3))
                step(dve.tensor_tensor(golden[:], golden[:], zone[:], ALU.mult))
                step(dve.tensor_reduce(gsum[:], golden[:], AX.X, ALU.add))
                step(dve.tensor_scalar(none_in[:], gsum[:], 1e-8, None, ALU.is_lt))
                fb_i = fallback[:].unsqueeze(3).to_broadcast([P, TPB, E, E])
                fb_j = fallback[:].unsqueeze(2).to_broadcast([P, TPB, E, E])
                step(dve.tensor_tensor(above, fb_j, fb_i, ALU.is_gt))
                step(dve.tensor_tensor(equal, fb_j, fb_i, ALU.is_equal))
                dve.wait_ge(s_const, 5)
                step(dve.tensor_tensor(equal, equal, earlier[:].unsqueeze(1).to_broadcast([P, TPB, E, E]), ALU.mult))
                step(dve.tensor_tensor(above, above, equal, ALU.add))
                step(dve.tensor_reduce(rank[:], above, AX.X, ALU.add))
                step(dve.scalar_tensor_tensor(out=fallback[:], in0=rank[:], scalar=2.0, in1=fallback[:],
                                              op0=ALU.is_lt, op1=ALU.mult))
                step(dve.tensor_reduce(fsum[:], fallback[:], AX.X, ALU.add))
                step(dve.tensor_scalar(fsum[:], fsum[:], 1e-8, None, ALU.max))
                step(dve.reciprocal(fsum[:], fsum[:]))
                step(dve.tensor_tensor(fsum[:], fsum[:], none_in[:], ALU.mult))
                step(dve.tensor_tensor(fallback[:], fallback[:], spread(fsum), ALU.mult))
                step(dve.tensor_scalar(none_in[:], none_in[:], -1.0, 1.0, ALU.mult, ALU.add))
                step(dve.tensor_tensor(golden[:], golden[:], spread(none_in), ALU.mult))
                step(dve.tensor_tensor(golden[:], golden[:], fallback[:], ALU.add))
                step(dve.tensor_reduce(gsum[:], golden[:], AX.X, ALU.add))
                step(dve.tensor_scalar(gsum[:], gsum[:], 1e-8, None, ALU.max))
                step(dve.reciprocal(gsum[:], gsum[:]))
                step(dve.tensor_tensor(combine[:, TPB * b:TPB * b + TPB, :], golden[:], spread(gsum), ALU.mult))
                assert done[0] == route_step.per_block

            def gated_up(n, f, parity):
                dve.wait_ge(silu_done.sem, silu_done.at(n, f + 1))
                dve.wait_ge(gu_done.sem, gu_done.at(n, f + 1))
                dve.tensor_tensor(h_raw[parity][:, f, :], gu_banks(n, f)[1][:], silu_g[:, parity, f, :], ALU.mult)\
                    .then_inc(hraw_done.sem, 1)

            def gated_ups(n, parity):
                dve.wait_ge(hlo_done.sem, hlo_done.before(n - 1))
                for f in range(C):
                    gated_up(n, f, parity)

            def accumulate(n, e, blk):
                dve.wait_ge(acc_done.sem, acc_done.before(n))
                for t in range(TPB):
                    if t % 2 == 0:
                        dve.wait_ge(down_done.sem, down_done.at(n, t // 2 + 1))
                    at = TPB * blk + t
                    weight = combine[:, at, e:e + 1] if isinstance(e, int) else combine[:, at, bass.ds(e, 1)]
                    dve.scalar_tensor_tensor(out=x_all[:, at, :], in0=down_bank(t // 2)[:, D * (t % 2):D * (t % 2) + D],
                                             scalar=weight, in1=x_all[:, at, :], op0=ALU.mult, op1=ALU.add)\
                        .then_inc(acc_done.sem, 1)

            dve.wait_ge(s_x0, 16)
            layernorm(0, 0)
            steps = [0]

            def setup(ins):
                steps[0] += 1
                ins.then_inc(s_setup, 1)
                dve.wait_ge(s_setup, steps[0])

            dve.wait_ge(s_vec, 32)
            setup(dve.scalar_tensor_tensor(out=sp[:, 0, :], in0=vec[:, :, 7], scalar=-1.0, in1=vec[:, :, 7],
                                           op0=ALU.mult, op1=ALU.max))
            normalize(0, 0)
            dve.wait_ge(s_wxy_hi, 1)
            dve.tensor_tensor(w_xy_lo[:].rearrange("p k n -> p (k n)"), w_raw[:, 0:C * 2 * D],
                              w_xy_hi[:].rearrange("p k n -> p (k n)").bitcast(F32), ALU.subtract).then_inc(s_wxy_lo, 1)
            rest_of_t(0, 0, x1t_hi, x1t_lo)
            setup(dve.reciprocal(inv_temp[:], temp[:]))
            dve.wait_ge(s_sp_act, 1)
            setup(dve.tensor_scalar(sp[:, 2, :], sp[:, 1, :], 2.0, None, ALU.add))
            setup(dve.reciprocal(sp[:, 2, :], sp[:, 2, :]))
            setup(dve.tensor_tensor(sp[:, 3, :], sp[:, 1, :], sp[:, 2, :], ALU.mult))
            setup(dve.tensor_tensor(sp[:, 4, :], sp[:, 3, :], sp[:, 3, :], ALU.mult))
            setup(dve.memset(sp[:, 2, :], 0.0))
            for k in range(ATANH_TERMS, 0, -1):
                setup(dve.scalar_tensor_tensor(out=sp[:, 2, :], in0=sp[:, 2, :], scalar=1.0 / (2 * k + 1),
                                               in1=sp[:, 4, :], op0=ALU.add, op1=ALU.mult))
            setup(dve.scalar_tensor_tensor(out=sp[:, 2, :], in0=sp[:, 2, :], scalar=1.0, in1=sp[:, 3, :],
                                           op0=ALU.add, op1=ALU.mult))
            setup(dve.tensor_scalar(sp[:, 4, :], vec[:, :, 7], 0.0, 8.0, ALU.max, ALU.mult))
            setup(dve.scalar_tensor_tensor(out=decay[:], in0=sp[:, 2, :], scalar=16.0, in1=sp[:, 4, :],
                                           op0=ALU.mult, op1=ALU.add))
            setup(dve.tensor_scalar(neg_decay[:], decay[:], -1.0, None, ALU.mult))
            assert steps[0] == SETUP_STEPS

            conv(0)
            for i in range(NB + 1):
                if i >= 1:
                    rest_of_t(1, i - 1, x2t_hi, x2t_lo)
                if i < NB - 1:
                    if i == 0:
                        dve.wait_ge(s_xrest, 16)
                    layernorm(0, i + 1)
                if i == 0:
                    for k in range(C):
                        dve.wait_ge(s_wvo_hi, k + 1)
                        dve.tensor_tensor(w_vo_lo[:, k, :], pS[k][:, 0:D], w_vo_hi[:, k, :].bitcast(F32),
                                          ALU.subtract).then_inc(s_wvo_lo, 1)
                if i == 0:
                    normalize(0, i + 1)
                    rest_of_t(0, i + 1, x1t_hi, x1t_lo)
                if i < NB:
                    multiplier_squared(i)
                if 0 < i < NB - 1:
                    normalize(0, i + 1)
                if i == NB:
                    gated_up(0, 0, 0)
                if i >= 3:
                    route_weights(i - 3)
                if i >= 2:
                    route_logits(i - 2)
                if i == NB:
                    route_distance(NB - 2)
                    route_weights(NB - 2)
                if i < NB:
                    scan(i)
                if 0 < i < NB - 1:
                    rest_of_t(0, i + 1, x1t_hi, x1t_lo)
                if i >= 1:
                    softmax_shift(i - 1)
                if 2 <= i < NB:
                    route_distance(i - 2)
                if i < NB - 1:
                    conv(i + 1)
                if i < NB:
                    x1(i)
                    layernorm(1, i)
                else:
                    gated_up(0, 1, 0)
                if i >= 1:
                    softmax_sum(i - 1)
                if i < NB:
                    normalize(1, i)
                if i >= 1:
                    x2(i - 1)
                    layernorm(2, i - 1)
                    normalize(2, i - 1)
            gated_up(1, 0, 1)
            accumulate(0, 0, 0)
            gated_up(1, 1, 1)
            route_logits(NB - 1)
            gated_ups(2, 0)
            accumulate(1, 0, 1)
            route_distance(NB - 1)
            route_weights(NB - 1)
            with dve.Fori(0, E // 2 - 1) as pair:
                for j in range(EARLY, EARLY + PAIR):
                    gated_ups(pair * PAIR + j, j % 2)
                    accumulate(pair * PAIR + (j - 1), pair * 2 + (j - 1) // STEPS, (j - 1) % STEPS)
            for n in range((E - 2) * STEPS + EARLY, E * STEPS + 1):
                if n < E * STEPS:
                    gated_ups(n, n % 2)
                accumulate(n - 1, (n - 1) // STEPS, (n - 1) % STEPS)


def lay_rows(w):
    return w.reshape(2, 128, -1).transpose(1, 0, 2)


def kernel(**inputs):
    import numpy as np
    import concourse.bacc as bacc
    from concourse.bass_utils import run_bass_kernel_spmd

    v = {n: np.asarray(a) for n, a in inputs.items()}
    B, S, d = v["x"].shape
    tokens = B * S

    def block_diagonal(w):
        out = np.zeros((2, 8, 16, 8, 16), w.dtype)
        for n in range(8):
            out[:, n, :, n, :] = w.reshape(2, 8, 16, 16)[:, n]
        return out.reshape(2, 128, 128).transpose(1, 0, 2)

    def flat(*parts):
        return np.ascontiguousarray(np.concatenate([p.reshape(128, -1) for p in parts], axis=1))

    def channels(a):
        return a.reshape(2, 128).T.reshape(128, 2, 1)

    w_stage1 = flat(block_diagonal(v["L0_attn_ig_w"]),
                    block_diagonal(v["L0_attn_ag_w"]), lay_rows(v["L0_attn_W_resid"].T))
    w_qko = flat(*(lay_rows(v[n].T) for n in ("L0_xattn_wq", "L0_xattn_wk", "L0_xattn_wo")))
    w_stage2 = flat(lay_rows(v["L0_xattn_wv"]), lay_rows(v["L0_ffn_Wr"]))
    vecs = np.ascontiguousarray(np.concatenate(
        [channels(v["L0_attn_conv_w"][i]) for i in range(4)]
        + [channels(v[n]) for n in ("L0_attn_conv_b", "L0_attn_ig_b", "L0_attn_ag_b", "L0_attn_a_param")], axis=2))
    experts = np.stack([v["L0_ffn_Wg"], v["L0_ffn_Wu"], v["L0_ffn_Wd"]], axis=1)
    experts = experts.reshape(experts.shape[0], 3, 2, 128, 256).transpose(0, 3, 1, 2, 4)
    ctx_t = v["ctx_2048"].reshape(tokens // BLK, BLK, 2, 128).transpose(0, 3, 2, 1)
    arrays = {
        "x": np.ascontiguousarray(v["x"].reshape(tokens, d)),
        "ctx_t": np.ascontiguousarray(ctx_t),
        "w_xy": flat(lay_rows(v["L0_attn_W_xy"].T)),
        "w_qko": w_qko,
        "w_stage1": w_stage1,
        "w_stage2": w_stage2,
        "channel_vecs": vecs,
        "w_experts": np.ascontiguousarray(experts).reshape(experts.shape[0], 128, -1),
        "temperature": np.ascontiguousarray(v["L0_ffn_temperature"]),
    }
    nc = bacc.Bacc("TRN2", target_bir_lowering=False, num_devices=1)
    args = [nc.dram_tensor(n, a.shape, mybir.dt.from_np(a.dtype), kind="ExternalInput").ap() for n, a in arrays.items()]
    out = nc.dram_tensor("out", (tokens, d), F32, kind="ExternalOutput").ap()
    decoder_kernel(nc, *args, out)
    result = run_bass_kernel_spmd(nc, [arrays], core_ids=[0])
    return result.results[0]["out"].reshape(B, S, d)
```

```python
from contextlib import ExitStack

import concourse.bass as bass
from concourse import mybir

ALU = mybir.AluOpType
ACT = mybir.ActivationFunctionType
AX = mybir.AxisListType
F32 = mybir.dt.float32
F32R = mybir.dt.float32r

P = 128
SEQ = 64
D = 256
C = D // P
BLK = 512
TPB = BLK // P
SPB = BLK // SEQ
CW = 4
PADDED = SEQ + CW - 1
SCALE = 1.0 / 16.0
EPS = 1e-5
GOLDEN_CENTER = 0.36787944117144233
GOLDEN_LOWER = 0.21231792754821915
GOLDEN_UPPER = 0.5
ATANH_TERMS = 9




class Tally:

    def __init__(self, sem, per_block, base=0):
        self.sem, self.per_block, self.base = sem, per_block, base

    def start(self, eng):
        eng.sem_inc(self.sem, self.base)

    def at(self, b, k):
        return b * self.per_block + (k + self.base)

    def before(self, b):
        return self.at(b, 0)


def decoder_kernel(nc, x, ctx, ctx_t, w_xy_d, w_qko_d, w_stage1, w_stage2, channel_vecs, w_experts, temperature, out):
    tokens = x.shape[0]
    NB = tokens // BLK
    NT = tokens // P
    E = w_experts.shape[0]
    WE = w_experts.shape[2]
    STEPS = NB
    PAIR = 2 * STEPS
    EARLY = 2
    LOOPED = 4

    x_tiles = x.rearrange("(t p) d -> p t d", p=P)
    ctx_tiles = ctx.rearrange("(t p) d -> p t d", p=P)
    out_tiles = out.rearrange("(t p) d -> p t d", p=P)

    with ExitStack() as stack:
        def sb(name, shape, dt=F32):
            return stack.enter_context(nc.sbuf_tensor(name, shape, dt))

        def sem(name):
            return stack.enter_context(nc.semaphore(name))

        def tally(name, per_block):
            return Tally(sem(name), per_block)

        def loop_tally(name, per_step):
            return Tally(sem(name), per_step, base=1)

        x_all = sb("x_all", [P, NT, D])
        x3t_hi = sb("x3t_hi", [P, C, tokens], F32R)
        x3t_lo = sb("x3t_lo", [P, C, tokens], F32R)
        combine = sb("combine", [P, NT, E])
        ident = sb("ident", [P, P])
        w_raw = sb("w_raw", [P, WE])
        w_hi = sb("w_hi", [P, 2, WE], F32R)
        w_lo = sb("w_lo", [P, 2, WE], F32R)
        w_xy_hi = sb("w_xy_hi", [P, C, 2 * D], F32R)
        w_xy_lo = sb("w_xy_lo", [P, C, 2 * D], F32R)
        w1 = sb("w1", [P, 2 * C * P + C * D])
        w_gates = w1[:, 0:2 * C * P].rearrange("p (g c n) -> p g c n", g=2, c=C)
        w_resid = w1[:, 2 * C * P:].rearrange("p (k n) -> p k n", k=C)
        w2 = sb("w2", [P, C * D + C * E])
        w_v = w2[:, 0:C * D].rearrange("p (k n) -> p k n", k=C)
        w_r = w2[:, C * D:].rearrange("p (k n) -> p k n", k=C)
        (w_q_hi, w_k_hi, w_o_hi), (w_q_lo, w_k_lo, w_o_lo) = (
            [w[:, 1, C * D * n:C * D * (n + 1)].rearrange("p (k n) -> p k n", k=C) for n in range(3)]
            for w in (w_hi, w_lo))
        w_v_hi = sb("w_v_hi", [P, C, D], F32R)
        w_v_lo = sb("w_v_lo", [P, C, D], F32R)
        vec = sb("vec", [P, C, 8])
        decay = sb("decay", [P, C])
        neg_decay = sb("neg_decay", [P, C])
        sp = sb("sp", [P, 5, C])
        temp = sb("temp", [P, 1])
        inv_temp = sb("inv_temp", [P, 1])
        exponent = sb("exponent", [P, TPB])
        earlier = sb("earlier", [P, E, E])
        stats = sb("stats", [P, 3, TPB, 6])
        mv = sb("mv", [P, 3, TPB, 2])
        var_eps = sb("var_eps", [P, 3, TPB])
        rstd = sb("rstd", [P, 3, TPB])
        xn = [sb(f"xn{n + 1}", [P, TPB, D]) for n in range(3)]
        h_hi = sb("h_hi", [P, 2, C, BLK], F32R)
        h_lo = sb("h_lo", [P, 2, C, BLK], F32R)
        x1t_hi, x1t_lo, x2t_hi, x2t_lo = h_hi[:, 0], h_lo[:, 0], h_hi[:, 1], h_lo[:, 1]
        xr_pad = sb("xr_pad", [P, C, SPB, PADDED])
        gelu_y = sb("gelu_y", [P, C, BLK])
        xc = sb("xc", [P, C, BLK])
        sig = sb("sig", [P, 2, C, BLK])
        gated = sb("gated", [P, C, BLK])
        a = sb("a", [P, C, BLK])
        tnh = sb("tnh", [P, C, BLK])
        mult = sb("mult", [P, C, BLK])
        h = sb("h", [P, C, BLK])
        ctxt = sb("ctxt", [P, C, BLK])
        v_ctx = sb("v_ctx", [P, TPB, D])
        qt = sb("qt", [P, C, BLK])
        knt = sb("knt", [P, C, BLK])
        v_new = sb("v_new", [P, TPB, D])
        smax = sb("smax", [P, TPB])
        ssum = sb("ssum", [P, TPB])
        sinv = sb("sinv", [P, TPB])
        probs = sb("probs", [P, TPB, 2, 2, SEQ])
        probs_t = sb("probs_t", [P, TPB, 2, P])
        ot_hi = sb("ot_hi", [P, C, BLK], F32R)
        ot_lo = sb("ot_lo", [P, C, BLK], F32R)
        x3t = sb("x3t", [P, C, BLK])
        inside, dist, zone, golden, fallback, rank = (sb(n, [P, TPB, E]) for n in (
            "inside", "dist", "zone", "golden", "fallback", "rank"))
        gsum, none_in, fsum = (sb(n, [P, TPB]) for n in ("gsum", "none_in", "fsum"))
        above, equal = (v[:, 0, 0:TPB * E * E].rearrange("p (t i j) -> p t i j", t=TPB, i=E) for v in (tnh, mult))
        silu_g = sig
        h_raw = [gated, a]

        banks = [stack.enter_context(nc.psum_tensor(f"bank{n}", [P, BLK], F32)) for n in range(8)]
        pT = banks[0:2]
        pA = banks[2:4]
        pB = banks[4:6]
        pS = banks[6:8]

        s_x0 = sem("x_block0_in")
        s_xrest = sem("x_rest_in")
        s_w1 = sem("w1_in")
        s_w2 = sem("w2_in")
        s_vec = sem("vec_in")
        s_out = sem("out_written")
        s_ctxt = sem("ctx_t_in")
        s_ctx = sem("ctx_rows_in")
        s_ident = sem("ident_ready")
        s_const = sem("const_ready")
        s_sp_act = sem("softplus_act")
        s_setup = sem("dve_setup")
        s_wv_hi = sem("w_v_hi_ready")
        s_wv_lo = sem("w_v_lo_ready")
        s_wxy_in = sem("raw_w_xy_in")
        s_wxy_hi = sem("w_xy_hi")
        s_wxy_lo = sem("w_xy_lo")
        s_landed = sem("raw_weights_in")
        pool_passed = sem("pool_waits_passed")
        ln_stats = [tally(f"ln{n + 1}_stats", TPB + 2) for n in range(3)]
        ln_rstd = [tally(f"ln{n + 1}_rstd", 1) for n in range(3)]
        ln_done = [tally(f"ln{n + 1}_done", TPB) for n in range(3)]
        t_done = [tally(f"t{n + 1}_done", C) for n in range(3)]
        t_hi = [tally(f"t{n + 1}_hi", C) for n in range(3)]
        t_lo = [tally(f"t{n + 1}_lo", C) for n in range(2)]
        tp_done = tally("probs_transposed", 2)
        tp_taken = tally("probs_t_taken", 2)
        xr_done = tally("xr_done", C)
        xr_taken = tally("xr_taken", C)
        y_done = tally("y_done", C)
        y_taken = tally("y_taken", C)
        conv_step = tally("conv_step", C * CW)
        gate_done = tally("gate_done", 4)
        gate_taken = tally("gate_taken", 4)
        gated_done = tally("gated_done", C)
        decay_done = tally("decay_done", 2 * C)
        square_done = tally("square_done", C)
        multsq_done = tally("multsq_done", C)
        sqrt_done = tally("sqrt_done", C)
        scan_step = tally("scan_step", 4 * C)
        resid_done = tally("resid_done", 2)
        x1_done = tally("x1_done", 2)
        o_done = tally("o_done", C)
        o_hi = tally("o_hi", C)
        o_lo = tally("o_lo", C)
        q_done = tally("q_done", C)
        q_taken = tally("q_taken", C)
        k_done = tally("k_done", C)
        k_taken = tally("k_taken", C)
        v_done = tally("v_done", 2)
        v_taken = tally("v_taken", 2)
        score_done = tally("score_done", 2)
        max_done = tally("max_done", 4)
        sub_done = tally("sub_done", 4)
        exp_done = tally("exp_done", 2)
        sum_done = tally("sum_done", 2)
        pv_done = tally("pv_done", 2)
        x2_done = tally("x2_done", TPB)
        router_done = tally("router_done", 1)
        logits_done = tally("logits_done", 1)
        route_step = tally("route_step", 25)
        route_act = tally("route_act", 3)
        split3 = tally("x3_split", 2 * C)
        gu_done = loop_tally("gate_up_done", C)
        silu_done = loop_tally("silu_done", C)
        hraw_done = loop_tally("h_done", C)
        hhi_done = loop_tally("h_hi_done", C)
        hlo_done = loop_tally("h_lo_done", C)
        down_done = loop_tally("down_done", 2)
        acc_done = loop_tally("acc_done", TPB)
        whi_done = loop_tally("w_hi_done", 1)
        wlo_done = loop_tally("w_lo_done", 1)
        QKO, EXPERT0 = 0, 1
        R_DIST, R_RANKED = 2, 13
        SETUP_STEPS = 7 + ATANH_TERMS + 4

        def xr_banks(b):
            return pB if b == 1 else pA

        def y_banks(b):
            return pS if b == 1 else pA

        def gu_banks(n, f):
            if isinstance(n, int) and n < EARLY:
                return banks[2], banks[3]
            return banks[2 * f], banks[2 * f + 1]

        def down_bank(half):
            return banks[4 + half]

        block = stack.enter_context(nc.Block())

        @block.sync
        def _(sp_eng):
            sp_eng.dma_start(x_all[:, 0:TPB, :], x_tiles[:, 0:TPB, :]).then_inc(s_x0, 16)
            sp_eng.dma_start(w_raw[:, 0:C * 2 * D], w_xy_d).then_inc(s_wxy_in, 16)
            sp_eng.dma_start(x_all[:, TPB:, :], x_tiles[:, TPB:, :]).then_inc(s_xrest, 16)
            sp_eng.wait_ge(s_wxy_lo, 1)
            sp_eng.dma_start(w_raw[:], w_qko_d).then_inc(s_landed, 16)
            sp_eng.dma_start(ctxt[:], ctx_t[0]).then_inc(s_ctxt, 16)
            sp_eng.dma_start(v_ctx[:], ctx_tiles[:, 0:TPB, :]).then_inc(s_ctx, 16)
            sp_eng.wait_ge(wlo_done.sem, wlo_done.before(EXPERT0))
            sp_eng.dma_start(w_raw[:], w_experts[0]).then_inc(s_landed, 16)
            for b in range(1, NB):
                sp_eng.wait_ge(score_done.sem, score_done.before(b))
                sp_eng.dma_start(ctxt[:], ctx_t[b]).then_inc(s_ctxt, 16)
                sp_eng.wait_ge(o_done.sem, o_done.before(b))
                sp_eng.dma_start(v_ctx[:], ctx_tiles[:, TPB * b:TPB * b + TPB, :]).then_inc(s_ctx, 16)
            with sp_eng.Fori(1, E) as e:
                sp_eng.wait_ge(wlo_done.sem, wlo_done.before(EXPERT0 + e))
                sp_eng.dma_start(w_raw[:], w_experts[bass.ds(e, 1)].rearrange("o p n -> (o p) n"))\
                    .then_inc(s_landed, 16)
            for b in range(NB):
                for half in range(2):
                    sp_eng.wait_ge(acc_done.sem, acc_done.at((E - 1) * STEPS + b, TPB // 2 * (half + 1)))
                    tiles = slice(TPB * b + TPB // 2 * half, TPB * b + TPB // 2 * (half + 1))
                    sp_eng.dma_start(out_tiles[:, tiles, :], x_all[:, tiles, :]).then_inc(s_out, 16)
            sp_eng.wait_ge(s_out, 16 * 2 * NB)

        @block.gpsimd
        def _(pool):
            for t in (hlo_done, whi_done, wlo_done):
                t.start(pool)
            pool.memset(exponent[:], -0.5).then_inc(s_const, 1)
            pool.memset(ident[:], 0.0).then_inc(s_ident, 1)
            pool.wait_ge(s_ident, 1)
            pool.affine_select(out=ident[:], in_=ident[:], compare_op=ALU.not_equal, fill=1.0, base=0,
                               pattern=[[-1, P]], channel_multiplier=1).then_inc(s_ident, 1)

            def split_landed(landing, n, hi, lo):
                pool.wait_ge(s_landed, landing * 16 + 16)
                pool.sem_inc(pool_passed, 1)
                pool.tensor_copy(hi, w_raw[:, 0:n]).then_inc(whi_done.sem, 1)
                pool.wait_ge(whi_done.sem, whi_done.at(landing, 1))
                pool.tensor_tensor(lo, w_raw[:, 0:n], hi.bitcast(F32), ALU.subtract).then_inc(wlo_done.sem, 1)

            def inverse_deviation(n, b):
                pool.wait_ge(ln_stats[n].sem, ln_stats[n].at(b, TPB + 2))
                pool.tensor_tensor(rstd[:, n, :], var_eps[:, n, :], exponent[:], ALU.pow).then_inc(ln_rstd[n].sem, 1)

            def input_gate(b, c):
                pool.wait_ge(conv_step.sem, conv_step.at(b, CW * (c + 1)))
                pool.wait_ge(gate_taken.sem, gate_taken.at(b, 2 * c + 1))
                if b > 0:
                    pool.wait_ge(scan_step.sem, scan_step.before(b))
                pool.tensor_tensor(gated[:, c, :], xc[:, c, :], sig[:, 0, c, :], ALU.mult)\
                    .then_inc(gated_done.sem, 1)

            def squares(b):
                for c in range(C):
                    pool.wait_ge(decay_done.sem, decay_done.at(b, c + 1))
                    pool.tensor_tensor(mult[:, c, :], a[:, c, :], a[:, c, :], ALU.mult).then_inc(square_done.sem, 1)

            def split_x3(b):
                cols = slice(BLK * b, BLK * b + BLK)
                for c in range(C):
                    pool.wait_ge(t_hi[2].sem, t_hi[2].at(b, c + 1))
                    if b < NB - 1:
                        pool.tensor_copy(x3t_hi[:, c, cols], x3t[:, c, :]).then_inc(split3.sem, 1)
                for c in range(C):
                    pool.wait_ge(split3.sem, split3.at(b, c + 1))
                    pool.tensor_tensor(x3t_lo[:, c, cols], x3t[:, c, :], x3t_hi[:, c, cols].bitcast(F32),
                                       ALU.subtract).then_inc(split3.sem, 1)

            def split_h(n, parity):
                for f in range(C):
                    pool.wait_ge(hraw_done.sem, hraw_done.at(n, f + 1))
                    pool.wait_ge(hhi_done.sem, hhi_done.at(n, f + 1))
                    pool.tensor_tensor(h_lo[:, parity, f, :], h_raw[parity][:, f, :],
                                       h_hi[:, parity, f, :].bitcast(F32), ALU.subtract).then_inc(hlo_done.sem, 1)

            def next_expert_lo(e, parity):
                pool.wait_ge(whi_done.sem, whi_done.at(EXPERT0 + e, 1))
                pool.tensor_tensor(w_lo[:, parity, :], w_raw[:], w_hi[:, parity, :].bitcast(F32), ALU.subtract)\
                    .then_inc(wlo_done.sem, 1)

            pool.memset(xr_pad[:], 0.0).then_inc(s_const, 1)
            inverse_deviation(0, 0)
            pool.memset(earlier[:], 1.0).then_inc(s_const, 1)
            pool.wait_ge(s_const, 3)
            pool.affine_select(out=earlier[:], in_=earlier[:], compare_op=ALU.is_gt, fill=0.0, base=0,
                               pattern=[[1, E], [-1, E]], channel_multiplier=0).then_inc(s_const, 1)
            pool.memset(probs[:], 0.0).then_inc(s_const, 1)
            input_gate(0, 0)
            for i in range(NB + 1):
                if i < NB:
                    input_gate(i, 1)
                if i <= 1:
                    inverse_deviation(0, i + 1)
                if i < NB:
                    squares(i)
                if i == 0:
                    pool.wait_ge(s_w2, 16)
                    pool.tensor_copy(w_v_hi[:], w_v[:]).then_inc(s_wv_hi, 1)
                    pool.wait_ge(s_wv_hi, 1)
                    pool.tensor_tensor(w_v_lo[:], w_v[:], w_v_hi[:].bitcast(F32), ALU.subtract).then_inc(s_wv_lo, 1)
                    split_landed(QKO, WE, w_hi[:, 1, :], w_lo[:, 1, :])
                if 1 < i < NB - 1:
                    inverse_deviation(0, i + 1)
                if i == 1:
                    split_landed(EXPERT0, WE, w_hi[:, 0, :], w_lo[:, 0, :])
                if i >= 2:
                    split_x3(i - 2)
                if i < NB:
                    inverse_deviation(1, i)
                else:
                    split_h(0, 0)
                if i < NB - 1:
                    input_gate(i + 1, 0)
                if i >= 1:
                    inverse_deviation(2, i - 1)
            next_expert_lo(1, 1)
            split_h(1, 1)
            split_x3(NB - 1)
            split_h(2, 0)
            split_h(3, 1)
            with pool.Fori(0, E // 2 - 1) as pair:
                for j in range(LOOPED, LOOPED + PAIR):
                    split_h(pair * PAIR + j, j % 2)
                    if j % STEPS == 0:
                        next_expert_lo(pair * 2 + 1 + j // STEPS, (j // STEPS + 1) % 2)
            for n in range((E - 2) * STEPS + LOOPED, E * STEPS):
                split_h(n, n % 2)

        @block.scalar
        def _(act):
            for t in (silu_done, hhi_done):
                t.start(act)
            act.dma_start(vec[:], channel_vecs).then_inc(s_vec, 16)
            act.dma_start(temp[:], temperature.partition_broadcast(P)).then_inc(s_vec, 16)
            act.dma_start(w1[:], w_stage1).then_inc(s_w1, 16)
            act.dma_start(w2[:], w_stage2).then_inc(s_w2, 16)
            act.wait_ge(s_setup, 1)
            act.activation(sp[:, 1, :], sp[:, 0, :], ACT.Exp, scale=-1.0).then_inc(s_sp_act, 1)
            act.wait_ge(s_wxy_in, 16)
            act.activation(w_xy_hi[:].rearrange("p k n -> p (k n)"), w_raw[:, 0:C * 2 * D], ACT.Copy).then_inc(s_wxy_hi, 1)

            def copy_out(b, psum, dst, ready, k, taken):
                act.wait_ge(ready.sem, ready.at(b, k + 1))
                act.activation(dst, psum, ACT.Copy).then_inc(taken.sem, 1)

            def take_t(n, b, dst):
                for c in range(C):
                    copy_out(b, pT[c][:], dst[:, c, :], t_done[n], c, t_hi[n])

            def take_x3t(b):
                if b > 0:
                    act.wait_ge(split3.sem, split3.before(b))
                take_t(2, b, x3t)
                if b == NB - 1:
                    for c in range(C):
                        act.wait_ge(t_hi[2].sem, t_hi[2].at(b, c + 1))
                        act.activation(x3t_hi[:, c, BLK * b:BLK * b + BLK], x3t[:, c, :], ACT.Copy).then_inc(split3.sem, 1)

            def take_xr(b):
                act.wait_ge(s_const, 2)
                if b > 0:
                    act.wait_ge(conv_step.sem, conv_step.before(b))
                for c in range(C):
                    copy_out(b, xr_banks(b)[c][:].rearrange("p (s t) -> p s t", s=SPB), xr_pad[:, c, :, CW - 1:PADDED],
                             xr_done, c, xr_taken)

            def gelus(b):
                if b > 0:
                    act.wait_ge(scan_step.sem, scan_step.before(b))
                for c in range(C):
                    act.wait_ge(y_done.sem, y_done.at(b, c + 1))
                    act.activation(gelu_y[:, c, :], y_banks(b)[c][:], ACT.Gelu).then_inc(y_taken.sem, 1)

            def sigmoids(b, c):
                if b > 0:
                    act.wait_ge(gated_done.sem, gated_done.before(b))
                for g in range(2):
                    act.wait_ge(gate_done.sem, gate_done.at(b, 2 * c + g + 1))
                    act.activation(sig[:, g, c, :], pA[g][:], ACT.Sigmoid,
                                   bias=vec[:, c, 5 + g:6 + g]).then_inc(gate_taken.sem, 1)

            def decays(b):
                act.wait_ge(s_setup, SETUP_STEPS)
                if b > 0:
                    act.wait_ge(scan_step.sem, scan_step.before(b))
                act.wait_ge(gate_taken.sem, gate_taken.at(b, 4))
                for c in range(C):
                    act.activation(a[:, c, :], sig[:, 1, c, :], ACT.Exp,
                                   scale=neg_decay[:, c:c + 1]).then_inc(decay_done.sem, 1)

            def tanhs(b):
                for c in range(C):
                    act.activation(tnh[:, c, :], sig[:, 1, c, :], ACT.Tanh,
                                   scale=decay[:, c:c + 1]).then_inc(decay_done.sem, 1)

            def roots(b):
                for c in range(C):
                    act.wait_ge(multsq_done.sem, multsq_done.at(b, c + 1))
                    act.activation(mult[:, c, :], tnh[:, c, :], ACT.Sqrt).then_inc(sqrt_done.sem, 1)

            def take_q(b):
                for n in range(C):
                    copy_out(b, pB[n][:], qt[:, n, :], q_done, n, q_taken)

            def take_k(b):
                for n in range(C):
                    copy_out(b, pS[n][:], knt[:, n, :], k_done, n, k_taken)

            def take_v(b, n):
                copy_out(b, pB[n][:].rearrange("p (t d) -> p t d", t=2), v_new[:, 2 * n:2 * n + 2, :], v_done, n, v_taken)

            def take_o(b):
                for c in range(C):
                    copy_out(b, pS[c][:], ot_hi[:, c, :], o_done, c, o_hi)

            def exponentials(b):
                for s in range(2):
                    act.wait_ge(sub_done.sem, sub_done.at(b, 4))
                    part = probs[SEQ * s:SEQ * s + SEQ, :, :, s, :]
                    act.activation(part, part, ACT.Exp, scale=SCALE).then_inc(exp_done.sem, 1)

            def take_tp(b):
                for n in range(2):
                    copy_out(b, pT[n][:].rearrange("p (t k q) -> p t k q", t=2, k=2),
                             probs_t[:, 2 * n:2 * n + 2, :, :], tp_done, n, tp_taken)

            def route_sigmoid(b):
                act.wait_ge(logits_done.sem, logits_done.at(b, 1))
                act.activation(inside[:], inside[:], ACT.Sigmoid).then_inc(route_act.sem, 1)

            def route_exponentials(b):
                act.wait_ge(route_step.sem, route_step.at(b, R_DIST))
                act.activation(golden[:], dist[:], ACT.Exp, scale=-10.0).then_inc(route_act.sem, 1)
                act.activation(fallback[:], dist[:], ACT.Exp, scale=-1.0 / 0.3).then_inc(route_act.sem, 1)

            def silu(n, f, parity):
                act.wait_ge(gu_done.sem, gu_done.at(n, f + 1))
                act.activation(silu_g[:, parity, f, :], gu_banks(n, f)[0][:], ACT.Silu).then_inc(silu_done.sem, 1)

            def expert_hi(e, parity):
                act.wait_ge(s_landed, (EXPERT0 + e) * 16 + 16)
                act.activation(w_hi[:, parity, :], w_raw[:], ACT.Copy).then_inc(whi_done.sem, 1)

            def next_expert_hi(e, parity):
                act.wait_ge(down_done.sem, down_done.at((e - 1) * STEPS - 1, 2))
                expert_hi(e, parity)

            def round_h(n, parity):
                for f in range(C):
                    act.wait_ge(hraw_done.sem, hraw_done.at(n, f + 1))
                    act.activation(h_hi[:, parity, f, :], h_raw[parity][:, f, :], ACT.Copy).then_inc(hhi_done.sem, 1)

            take_t(0, 0, x1t_hi)
            take_xr(0)
            for i in range(NB + 1):
                if i < NB:
                    sigmoids(i, 0)
                if i >= 1:
                    take_t(1, i - 1, x2t_hi)
                if i < NB:
                    sigmoids(i, 1)
                if i < NB:
                    decays(i)
                    tanhs(i)
                else:
                    silu(0, 0, 0)
                if i == 0:
                    take_t(0, 1, x1t_hi)
                if 2 <= i < NB:
                    take_x3t(i - 2)
                if i == 1:
                    take_q(0)
                if i < NB:
                    roots(i)
                if i < NB and i != 1:
                    gelus(i)
                if i == 0:
                    take_xr(1)
                    gelus(1)
                if i > 1:
                    take_q(i - 1)
                if 2 <= i < NB - 1:
                    take_t(0, i + 1, x1t_hi)
                if i >= 1:
                    take_k(i - 1)
                if i == 1:
                    take_t(0, 2, x1t_hi)
                if i == NB:
                    take_x3t(NB - 2)
                if i >= 1:
                    take_v(i - 1, 0)
                if 2 <= i < NB:
                    route_sigmoid(i - 2)
                if 0 < i < NB - 1:
                    take_xr(i + 1)
                if i == NB:
                    route_exponentials(NB - 3)
                if i >= 1:
                    exponentials(i - 1)
                if 2 <= i < NB - 1:
                    route_exponentials(i - 2)
                if i == NB:
                    silu(0, 1, 0)
                if i >= 1:
                    take_tp(i - 1)
                    take_v(i - 1, 1)
                if i == NB:
                    round_h(0, 0)
                if i >= 1:
                    take_o(i - 1)
            silu(1, 0, 1)
            act.wait_ge(pv_done.sem, pv_done.at(NB - 1, 2))
            expert_hi(1, 1)
            silu(1, 1, 1)
            take_x3t(NB - 1)
            route_sigmoid(NB - 2)
            round_h(1, 1)
            route_exponentials(NB - 2)
            silu(2, 0, 0)
            silu(2, 1, 0)
            round_h(2, 0)
            silu(3, 0, 1)
            silu(3, 1, 1)
            route_sigmoid(NB - 1)
            round_h(3, 1)
            route_exponentials(NB - 1)
            with act.Fori(0, E // 2 - 1) as pair:
                for j in range(LOOPED, LOOPED + PAIR):
                    for f in range(C):
                        silu(pair * PAIR + j, f, j % 2)
                    round_h(pair * PAIR + j, j % 2)
                    if j % STEPS == 0:
                        next_expert_hi(pair * 2 + 1 + j // STEPS, (j // STEPS + 1) % 2)
            for n in range((E - 2) * STEPS + LOOPED, E * STEPS):
                for f in range(C):
                    silu(n, f, n % 2)
                round_h(n, n % 2)

        @block.tensor
        def _(pe):
            for t in (gu_done, down_done):
                t.start(pe)

            def product(dst, lhs, rhs, done=None):
                for k in range(C):
                    last = pe.matmul(dst, lhs(k), rhs(k), start=(k == 0), stop=(k == C - 1))
                if done is not None:
                    last.then_inc(done.sem, 1)

            def split_product(dst, lhs_hi, lhs_lo, rhs_hi, rhs_lo, done=None):
                n = 0
                for k in range(C):
                    for p, q in ((lhs_hi, rhs_hi), (lhs_hi, rhs_lo), (lhs_lo, rhs_hi)):
                        last = pe.matmul(dst, p(k), q(k), start=(n == 0), stop=(n == 3 * C - 1))
                        n += 1
                if done is not None:
                    last.then_inc(done.sem, 1)

            def transposes(n, b):
                for c in range(C):
                    for t in range(TPB):
                        if c == 0:
                            pe.wait_ge(ln_done[n].sem, ln_done[n].at(b, t + 1))
                        last = pe.transpose(pT[c][:, P * t:P * t + P], xn[n][:, t, P * c:P * c + P], ident[:])
                    last.then_inc(t_done[n].sem, 1)

            def xr(b):
                pe.wait_ge(t_lo[0].sem, t_lo[0].at(b, C))
                for n in range(C):
                    if b == 2:
                        pe.wait_ge(gate_taken.sem, gate_taken.at(b - 1, C + n + 1))
                    elif b > 2:
                        pe.wait_ge(y_taken.sem, y_taken.at(b - 1, n + 1))
                    cols = slice(P * n, P * n + P)
                    split_product(xr_banks(b)[n][:], lambda k: w_xy_hi[:, k, cols], lambda k: w_xy_lo[:, k, cols],
                                  lambda k: x1t_hi[:, k, :], lambda k: x1t_lo[:, k, :], xr_done)

            def y(b):
                for n in range(C):
                    if b != 1:
                        pe.wait_ge(gate_taken.sem, gate_taken.at(b, C + n + 1))
                    cols = slice(D + P * n, D + P * n + P)
                    split_product(y_banks(b)[n][:], lambda k: w_xy_hi[:, k, cols], lambda k: w_xy_lo[:, k, cols],
                                  lambda k: x1t_hi[:, k, :], lambda k: x1t_lo[:, k, :], y_done)

            def gates(b, c):
                pe.wait_ge(conv_step.sem, conv_step.at(b, CW * (c + 1)))
                for g in range(2):
                    if c > 0:
                        pe.wait_ge(gate_taken.sem, gate_taken.at(b, g + 1))
                    elif b > 0:
                        pe.wait_ge(x1_done.sem, x1_done.at(b - 1, g + 1))
                    else:
                        pe.wait_ge(xr_taken.sem, xr_taken.at(b, g + 1))
                    pe.matmul(pA[g][:], w_gates[:, g, c, :], xc[:, c, :], start=True, stop=True)\
                        .then_inc(gate_done.sem, 1)

            def resid(b):
                pe.wait_ge(scan_step.sem, scan_step.at(b, 4 * C))
                for t in range(TPB):
                    if 0 < b < NB - 1:
                        pe.wait_ge(xr_taken.sem, xr_taken.at(b + 1, t // 2 + 1))
                    else:
                        pe.wait_ge(y_taken.sem, y_taken.at(b, t // 2 + 1))
                    dst = pA[t // 2][:, D * (t % 2):D * (t % 2) + D]
                    product(dst, lambda k: h[:, k, P * t:P * t + P], lambda k: w_resid[:, k, :],
                            resid_done if t % 2 else None)

            def queries(b):
                pe.wait_ge(t_lo[1].sem, t_lo[1].at(b, C))
                if b > 0:
                    pe.wait_ge(v_taken.sem, v_taken.before(b))
                else:
                    pe.wait_ge(xr_taken.sem, xr_taken.at(1, C))
                for n in range(C):
                    cols = slice(P * n, P * n + P)
                    split_product(pB[n][:], lambda k: w_q_hi[:, k, cols], lambda k: w_q_lo[:, k, cols],
                                  lambda k: x2t_hi[:, k, :], lambda k: x2t_lo[:, k, :], q_done)

            def keys(b):
                if b > 0:
                    pe.wait_ge(x2_done.sem, x2_done.before(b))
                    pe.wait_ge(logits_done.sem, logits_done.before(min(b, NB - 2)))
                else:
                    pe.wait_ge(y_taken.sem, y_taken.at(1, C))
                for n in range(C):
                    cols = slice(P * n, P * n + P)
                    split_product(pS[n][:], lambda k: w_k_hi[:, k, cols], lambda k: w_k_lo[:, k, cols],
                                  lambda k: x2t_hi[:, k, :], lambda k: x2t_lo[:, k, :], k_done)

            def values(b, n):
                pe.wait_ge(q_taken.sem, q_taken.at(b, n + 1))
                for u in range(2):
                    tile = slice(P * (2 * n + u), P * (2 * n + u) + P)
                    split_product(pB[n][:, D * u:D * u + D], lambda k: x2t_hi[:, k, tile], lambda k: x2t_lo[:, k, tile],
                                  lambda k: w_v_hi[:, k, :], lambda k: w_v_lo[:, k, :], v_done if u else None)

            def scores(b):
                pe.wait_ge(s_ctxt, 16 * b + 16)
                pe.wait_ge(q_taken.sem, q_taken.at(b, C))
                pe.wait_ge(k_taken.sem, k_taken.at(b, C))
                for t in range(TPB):
                    pair = slice(P * t, P * t + P)
                    for m, key in enumerate((ctxt, knt)):
                        at = D * (t % 2) + P * m
                        for k in range(C):
                            last = pe.matmul(pS[t // 2][:, at:at + P], qt[:, k, pair], key[:, k, pair],
                                             start=(k == 0), stop=(k == C - 1))
                    if t % 2:
                        last.then_inc(score_done.sem, 1)

            def probs_transpose(b):
                pe.wait_ge(exp_done.sem, exp_done.at(b, 2))
                for t in range(TPB):
                    for m in range(2):
                        at = D * (t % 2) + P * m
                        last = pe.transpose(pT[t // 2][:, at:at + P],
                                            probs[:, t, m, :, :].rearrange("p s k -> p (s k)"), ident[:])
                    if t % 2:
                        last.then_inc(tp_done.sem, 1)

            def attend(b):
                pe.wait_ge(s_ctx, 16 * b + 16)
                pe.wait_ge(sub_done.sem, sub_done.at(b, 4))
                if b == NB - 1:
                    pe.wait_ge(logits_done.sem, logits_done.at(NB - 2, 1))
                for c in range(C):
                    for t in range(TPB):
                        if c == 0:
                            pe.wait_ge(tp_taken.sem, tp_taken.at(b, t // 2 + 1))
                            pe.wait_ge(v_taken.sem, v_taken.at(b, t // 2 + 1))
                        for m, v in enumerate((v_ctx, v_new)):
                            last = pe.matmul(pS[c][:, P * t:P * t + P], v[:, t, P * c:P * c + P], probs_t[:, t, m, :],
                                             start=(m == 0), stop=(m == 1))
                    last.then_inc(o_done.sem, 1)

            def project(b):
                pe.wait_ge(o_lo.sem, o_lo.at(b, C))
                for t in range(TPB):
                    tile = slice(P * t, P * t + P)
                    split_product(pS[t // 2][:, D * (t % 2):D * (t % 2) + D], lambda k: ot_hi[:, k, tile],
                                  lambda k: ot_lo[:, k, tile], lambda k: w_o_hi[:, k, :], lambda k: w_o_lo[:, k, :],
                                  pv_done if t % 2 else None)

            def router(b):
                pe.wait_ge(t_hi[2].sem, t_hi[2].at(b, C))
                if b == NB - 2:
                    pe.wait_ge(sub_done.sem, sub_done.at(NB - 1, 4))
                else:
                    pe.wait_ge(x2_done.sem, x2_done.at(b, TPB))
                for t in range(TPB):
                    product(pS[0][:, E * t:E * t + E], lambda k: x3t[:, k, P * t:P * t + P], lambda k: w_r[:, k, :],
                            router_done if t == TPB - 1 else None)

            def gate_up(n, j, f):
                par, cols = (j // STEPS) % 2, slice(BLK * (j % STEPS), BLK * (j % STEPS) + BLK)
                for which in range(2):
                    def at(k):
                        start = (which * C + k) * D + P * f
                        return slice(start, start + P)
                    split_product(gu_banks(n, f)[which][:], lambda k: w_hi[:, par, at(k)], lambda k: w_lo[:, par, at(k)],
                                  lambda k: x3t_hi[:, k, cols], lambda k: x3t_lo[:, k, cols],
                                  gu_done if which else None)

            def gate_ups(n, j):
                for f in range(C):
                    pe.wait_ge(hraw_done.sem, hraw_done.at(n - 1, f + 1))
                    gate_up(n, j, f)

            def down(n, j):
                par = (j // STEPS) % 2
                pe.wait_ge(acc_done.sem, acc_done.before(n))
                pe.wait_ge(hlo_done.sem, hlo_done.at(n, C))
                for t in range(TPB):
                    def rows(f):
                        start = (2 * C + f) * D
                        return slice(start, start + D)
                    tile = slice(P * t, P * t + P)
                    split_product(down_bank(t // 2)[:, D * (t % 2):D * (t % 2) + D],
                                  lambda f: h_hi[:, j % 2, f, tile], lambda f: h_lo[:, j % 2, f, tile],
                                  lambda f: w_hi[:, par, rows(f)], lambda f: w_lo[:, par, rows(f)],
                                  down_done if t % 2 else None)

            pe.wait_ge(s_ident, 2)
            transposes(0, 0)
            pe.wait_ge(s_wxy_lo, 1)
            xr(0)
            pe.wait_ge(s_w1, 16)
            gates(0, 0)
            for i in range(NB + 1):
                if i < NB:
                    gates(i, 1)
                if i < NB and i != 1:
                    y(i)
                if 2 <= i < NB:
                    pe.wait_ge(t_lo[1].sem, t_lo[1].at(i - 1, C))
                    transposes(2, i - 2)
                if i == 1:
                    pe.wait_ge(wlo_done.sem, wlo_done.at(QKO, 1))
                    pe.wait_ge(s_wv_lo, 1)
                if i >= 1:
                    queries(i - 1)
                if 2 <= i < NB:
                    router(i - 2)
                if 2 <= i < NB - 1:
                    transposes(0, i + 1)
                if i >= 1:
                    keys(i - 1)
                if i <= 1:
                    transposes(0, i + 1)
                if i == NB:
                    transposes(2, NB - 2)
                if i >= 1:
                    values(i - 1, 0)
                    scores(i - 1)
                if i < NB - 1:
                    xr(i + 1)
                if i == 0:
                    y(1)
                if i < NB:
                    resid(i)
                else:
                    pe.wait_ge(hraw_done.sem, hraw_done.at(0, 1))
                    gate_up(0, 0, 1)
                    router(NB - 2)
                if i >= 1:
                    probs_transpose(i - 1)
                    values(i - 1, 1)
                    attend(i - 1)
                if i < NB - 1:
                    gates(i + 1, 0)
                elif i == NB - 1:
                    pe.wait_ge(wlo_done.sem, wlo_done.at(EXPERT0, 1))
                    pe.wait_ge(x1_done.sem, x1_done.at(NB - 1, 2))
                    gate_up(0, 0, 0)
                else:
                    pe.wait_ge(hraw_done.sem, hraw_done.at(0, C))
                    gate_up(1, 1, 0)
                if i < NB:
                    transposes(1, i)
                if i >= 1:
                    project(i - 1)
            down(0, 0)
            pe.wait_ge(hraw_done.sem, hraw_done.at(1, 1))
            gate_up(1, 1, 1)
            transposes(2, NB - 1)
            pe.wait_ge(t_hi[2].sem, t_hi[2].at(NB - 1, C))
            pe.wait_ge(hraw_done.sem, hraw_done.at(1, C))
            gate_up(2, 2, 0)
            router(NB - 1)
            gate_up(2, 2, 1)
            down(1, 1)
            pe.wait_ge(split3.sem, split3.at(NB - 1, 2 * C))
            gate_ups(3, 3)
            down(2, 2)
            with pe.Fori(0, E // 2 - 1) as pair:
                for j in range(LOOPED, LOOPED + PAIR):
                    if j % STEPS == 0:
                        pe.wait_ge(wlo_done.sem, wlo_done.at(pair * 2 + (EXPERT0 + j // STEPS), 1))
                    gate_ups(pair * PAIR + j, j)
                    down(pair * PAIR + (j - 1), j - 1)
            for n in range((E - 2) * STEPS + LOOPED, E * STEPS + 1):
                if n < E * STEPS:
                    if n % STEPS == 0:
                        pe.wait_ge(wlo_done.sem, wlo_done.at(EXPERT0 + n // STEPS, 1))
                    gate_ups(n, n)
                down(n - 1, n - 1)

        @block.vector
        def _(dve):
            for t in (hraw_done, acc_done):
                t.start(dve)

            def layernorm(n, b):
                if b > 0:
                    dve.wait_ge(t_done[n].sem, t_done[n].before(b))
                if n:
                    dve.wait_ge((x1_done, x2_done)[n - 1].sem, (x1_done, x2_done)[n - 1].at(b, (2, TPB)[n - 1]))
                for t in range(TPB):
                    dve.bn_stats(stats[:, n, t, :], x_all[:, TPB * b + t, :]).then_inc(ln_stats[n].sem, 1)
                for t in range(TPB):
                    dve.wait_ge(ln_stats[n].sem, ln_stats[n].at(b, t + 1))
                    ins = dve.bn_aggr(mv[:, n, t, :], stats[:, n, t, :])
                ins.then_inc(ln_stats[n].sem, 1)
                dve.wait_ge(ln_stats[n].sem, ln_stats[n].at(b, TPB + 1))
                dve.tensor_scalar(var_eps[:, n, :], mv[:, n, :, 1], EPS, None, ALU.add).then_inc(ln_stats[n].sem, 1)

            def normalize(n, b):
                dve.wait_ge(ln_rstd[n].sem, ln_rstd[n].at(b, 1))
                for t in range(TPB):
                    dve.tensor_scalar(xn[n][:, t, :], x_all[:, TPB * b + t, :], mv[:, n, t, 0:1], rstd[:, n, t:t + 1],
                                      ALU.subtract, ALU.mult).then_inc(ln_done[n].sem, 1)

            def rest_of_t(n, b, hi, lo):
                for c in range(C):
                    dve.wait_ge(t_hi[n].sem, t_hi[n].at(b, c + 1))
                    dve.tensor_tensor(lo[:, c, :], pT[c][:], hi[:, c, :].bitcast(F32), ALU.subtract)\
                        .then_inc(t_lo[n].sem, 1)

            def conv(b, c):
                if b > 0:
                    dve.wait_ge(gate_done.sem, gate_done.before(b))
                    dve.wait_ge(gated_done.sem, gated_done.before(b))
                dve.wait_ge(xr_taken.sem, xr_taken.at(b, c + 1))
                view = xc[:, c, :].rearrange("p (s t) -> p s t", s=SPB)
                for i in range(CW):
                    src = xr_pad[:, c, :, i:i + SEQ]
                    if i == 0:
                        ins = dve.tensor_scalar(view, src, vec[:, c, 0:1], vec[:, c, 4:5], ALU.mult, ALU.add)
                    else:
                        dve.wait_ge(conv_step.sem, conv_step.at(b, CW * c + i))
                        ins = dve.scalar_tensor_tensor(out=view, in0=src, scalar=vec[:, c, i:i + 1], in1=view,
                                                       op0=ALU.mult, op1=ALU.add)
                    ins.then_inc(conv_step.sem, 1)

            def multiplier_squared(b):
                for c in range(C):
                    dve.wait_ge(square_done.sem, square_done.at(b, c + 1))
                    dve.wait_ge(decay_done.sem, decay_done.at(b, C + c + 1))
                    dve.scalar_tensor_tensor(out=tnh[:, c, :], in0=mult[:, c, :], scalar=1.0, in1=tnh[:, c, :],
                                             op0=ALU.add, op1=ALU.mult).then_inc(multsq_done.sem, 1)

            def scan(b):
                if b > 0:
                    dve.wait_ge(resid_done.sem, resid_done.before(b))
                for c in range(C):
                    dve.wait_ge(square_done.sem, square_done.at(b, c + 1))
                    dve.memset(a[:, c, :].rearrange("p (s t) -> p s t", s=SPB)[:, :, 0:1], 0.0)\
                        .then_inc(scan_step.sem, 1)
                    dve.wait_ge(sqrt_done.sem, sqrt_done.at(b, c + 1))
                    dve.wait_ge(gated_done.sem, gated_done.at(b, c + 1))
                    dve.tensor_tensor(h[:, c, :], gated[:, c, :], mult[:, c, :], ALU.mult).then_inc(scan_step.sem, 1)
                    dve.wait_ge(scan_step.sem, scan_step.at(b, 4 * c + 2))
                    dve.tensor_tensor_scan(h[:, c, :], a[:, c, :], h[:, c, :], 0.0, ALU.mult, ALU.add)\
                        .then_inc(scan_step.sem, 1)
                    dve.wait_ge(scan_step.sem, scan_step.at(b, 4 * c + 3))
                    dve.wait_ge(y_taken.sem, y_taken.at(b, c + 1))
                    dve.tensor_tensor(h[:, c, :], h[:, c, :], gelu_y[:, c, :], ALU.mult).then_inc(scan_step.sem, 1)

            def x1(b):
                for n in range(2):
                    dve.wait_ge(resid_done.sem, resid_done.at(b, n + 1))
                    tiles = x_all[:, TPB * b + 2 * n:TPB * b + 2 * n + 2, :]
                    dve.tensor_tensor(tiles, pA[n][:].rearrange("p (t d) -> p t d", t=2), tiles, ALU.add)\
                        .then_inc(x1_done.sem, 1)

            def softmax_shift(b):
                def own(n, s):
                    return pS[n][SEQ * s:SEQ * s + SEQ, :].rearrange("p (t m s k) -> p t m s k", t=2, m=2, s=2)[:, :, :, s, :]
                for n in range(2):
                    dve.wait_ge(score_done.sem, score_done.at(b, n + 1))
                    for s in range(2):
                        dve.tensor_reduce(smax[SEQ * s:SEQ * s + SEQ, 2 * n:2 * n + 2], own(n, s), AX.XY, ALU.max)\
                            .then_inc(max_done.sem, 1)
                for n in range(2):
                    for s in range(2):
                        dve.wait_ge(max_done.sem, max_done.at(b, 2 * n + s + 1))
                        rows = slice(SEQ * s, SEQ * s + SEQ)
                        for u in range(2):
                            t = 2 * n + u
                            ins = dve.tensor_scalar(probs[rows, t, :, s, :], own(n, s)[:, u, :, :],
                                                    smax[rows, t:t + 1], None, ALU.subtract)
                        ins.then_inc(sub_done.sem, 1)

            def softmax_sum(b):
                dve.wait_ge(exp_done.sem, exp_done.at(b, 2))
                dve.tensor_reduce(ssum[:], probs[:].rearrange("p t m s k -> p t (m s k)"), AX.X, ALU.add)\
                    .then_inc(sum_done.sem, 1)
                dve.wait_ge(sum_done.sem, sum_done.at(b, 1))
                dve.reciprocal(sinv[:], ssum[:]).then_inc(sum_done.sem, 1)

            def rest_of_o(b):
                for c in range(C):
                    dve.wait_ge(o_hi.sem, o_hi.at(b, c + 1))
                    dve.tensor_tensor(ot_lo[:, c, :], pS[c][:], ot_hi[:, c, :].bitcast(F32), ALU.subtract)\
                        .then_inc(o_lo.sem, 1)

            def x2(b):
                dve.wait_ge(sum_done.sem, sum_done.at(b, 2))
                for t in range(TPB):
                    if t % 2 == 0:
                        dve.wait_ge(pv_done.sem, pv_done.at(b, t // 2 + 1))
                    tile = x_all[:, TPB * b + t, :]
                    dve.scalar_tensor_tensor(out=tile, in0=pS[t // 2][:, D * (t % 2):D * (t % 2) + D],
                                             scalar=sinv[:, t:t + 1], in1=tile, op0=ALU.mult, op1=ALU.add)\
                        .then_inc(x2_done.sem, 1)

            def route_logits(b):
                dve.wait_ge(router_done.sem, router_done.at(b, 1))
                dve.tensor_scalar(inside[:], pS[0][:, 0:TPB * E].rearrange("p (t e) -> p t e", t=TPB),
                                  inv_temp[:, 0:1], None, ALU.mult).then_inc(logits_done.sem, 1)

            def route_distance(b):
                dve.wait_ge(route_act.sem, route_act.at(b, 1))
                dve.tensor_scalar(zone[:], inside[:], GOLDEN_CENTER, None, ALU.subtract).then_inc(route_step.sem, 1)
                dve.wait_ge(route_step.sem, route_step.at(b, 1))
                dve.scalar_tensor_tensor(out=dist[:], in0=zone[:], scalar=-1.0, in1=zone[:], op0=ALU.mult,
                                         op1=ALU.max).then_inc(route_step.sem, 1)
                dve.wait_ge(route_step.sem, route_step.at(b, R_DIST))
                dve.tensor_scalar(zone[:], inside[:], GOLDEN_UPPER, None, ALU.is_le).then_inc(route_step.sem, 1)
                dve.wait_ge(route_step.sem, route_step.at(b, R_DIST + 1))
                dve.scalar_tensor_tensor(out=zone[:], in0=inside[:], scalar=GOLDEN_LOWER, in1=zone[:],
                                         op0=ALU.is_ge, op1=ALU.mult).then_inc(route_step.sem, 1)

            def spread(v):
                return v[:].unsqueeze(2).to_broadcast([P, TPB, E])

            def route_ranks(b):
                done = [R_DIST + 2]

                def step(ins):
                    done[0] += 1
                    ins.then_inc(route_step.sem, 1)
                    dve.wait_ge(route_step.sem, route_step.at(b, done[0]))

                fb_i = fallback[:].unsqueeze(3).to_broadcast([P, TPB, E, E])
                fb_j = fallback[:].unsqueeze(2).to_broadcast([P, TPB, E, E])
                dve.wait_ge(route_act.sem, route_act.at(b, 3))
                dve.wait_ge(route_step.sem, route_step.at(b, R_DIST + 2))
                step(dve.tensor_tensor(golden[:], golden[:], zone[:], ALU.mult))
                step(dve.tensor_reduce(gsum[:], golden[:], AX.X, ALU.add))
                step(dve.tensor_scalar(none_in[:], gsum[:], 1e-8, None, ALU.is_lt))
                step(dve.tensor_tensor(above, fb_j, fb_i, ALU.is_gt))
                step(dve.tensor_tensor(equal, fb_j, fb_i, ALU.is_equal))
                dve.wait_ge(s_const, 5)
                step(dve.tensor_tensor(equal, equal, earlier[:].unsqueeze(1).to_broadcast([P, TPB, E, E]), ALU.mult))
                step(dve.tensor_tensor(above, above, equal, ALU.add))
                step(dve.tensor_reduce(rank[:], above, AX.X, ALU.add))
                step(dve.scalar_tensor_tensor(out=fallback[:], in0=rank[:], scalar=2.0, in1=fallback[:],
                                              op0=ALU.is_lt, op1=ALU.mult))
                assert done[0] == R_RANKED

            def route_weights(b):
                done = [R_RANKED]

                def step(ins):
                    done[0] += 1
                    ins.then_inc(route_step.sem, 1)
                    dve.wait_ge(route_step.sem, route_step.at(b, done[0]))

                step(dve.tensor_reduce(fsum[:], fallback[:], AX.X, ALU.add))
                step(dve.tensor_scalar(fsum[:], fsum[:], 1e-8, None, ALU.max))
                step(dve.reciprocal(fsum[:], fsum[:]))
                step(dve.tensor_tensor(fsum[:], fsum[:], none_in[:], ALU.mult))
                step(dve.tensor_tensor(fallback[:], fallback[:], spread(fsum), ALU.mult))
                step(dve.tensor_scalar(none_in[:], none_in[:], -1.0, 1.0, ALU.mult, ALU.add))
                step(dve.tensor_tensor(golden[:], golden[:], spread(none_in), ALU.mult))
                step(dve.tensor_tensor(golden[:], golden[:], fallback[:], ALU.add))
                step(dve.tensor_reduce(gsum[:], golden[:], AX.X, ALU.add))
                step(dve.tensor_scalar(gsum[:], gsum[:], 1e-8, None, ALU.max))
                step(dve.reciprocal(gsum[:], gsum[:]))
                step(dve.tensor_tensor(combine[:, TPB * b:TPB * b + TPB, :], golden[:], spread(gsum), ALU.mult))
                assert done[0] == route_step.per_block

            def gated_up(n, f, parity):
                dve.wait_ge(silu_done.sem, silu_done.at(n, f + 1))
                dve.wait_ge(gu_done.sem, gu_done.at(n, f + 1))
                dve.tensor_tensor(h_raw[parity][:, f, :], gu_banks(n, f)[1][:], silu_g[:, parity, f, :], ALU.mult)\
                    .then_inc(hraw_done.sem, 1)

            def gated_ups(n, parity):
                dve.wait_ge(hlo_done.sem, hlo_done.before(n - 1))
                for f in range(C):
                    gated_up(n, f, parity)

            def accumulate(n, e, blk):
                dve.wait_ge(acc_done.sem, acc_done.before(n))
                for t in range(TPB):
                    if t % 2 == 0:
                        dve.wait_ge(down_done.sem, down_done.at(n, t // 2 + 1))
                    at = TPB * blk + t
                    weight = combine[:, at, e:e + 1] if isinstance(e, int) else combine[:, at, bass.ds(e, 1)]
                    dve.scalar_tensor_tensor(out=x_all[:, at, :], in0=down_bank(t // 2)[:, D * (t % 2):D * (t % 2) + D],
                                             scalar=weight, in1=x_all[:, at, :], op0=ALU.mult, op1=ALU.add)\
                        .then_inc(acc_done.sem, 1)

            dve.wait_ge(s_x0, 16)
            layernorm(0, 0)
            steps = [0]

            def setup(ins):
                steps[0] += 1
                ins.then_inc(s_setup, 1)
                dve.wait_ge(s_setup, steps[0])

            dve.wait_ge(s_vec, 32)
            setup(dve.scalar_tensor_tensor(out=sp[:, 0, :], in0=vec[:, :, 7], scalar=-1.0, in1=vec[:, :, 7],
                                           op0=ALU.mult, op1=ALU.max))
            normalize(0, 0)
            dve.wait_ge(s_wxy_hi, 1)
            dve.tensor_tensor(w_xy_lo[:].rearrange("p k n -> p (k n)"), w_raw[:, 0:C * 2 * D],
                              w_xy_hi[:].rearrange("p k n -> p (k n)").bitcast(F32), ALU.subtract).then_inc(s_wxy_lo, 1)
            rest_of_t(0, 0, x1t_hi, x1t_lo)
            setup(dve.reciprocal(inv_temp[:], temp[:]))
            dve.wait_ge(s_sp_act, 1)
            setup(dve.tensor_scalar(sp[:, 2, :], sp[:, 1, :], 2.0, None, ALU.add))
            setup(dve.reciprocal(sp[:, 2, :], sp[:, 2, :]))
            setup(dve.tensor_tensor(sp[:, 3, :], sp[:, 1, :], sp[:, 2, :], ALU.mult))
            setup(dve.tensor_tensor(sp[:, 4, :], sp[:, 3, :], sp[:, 3, :], ALU.mult))
            setup(dve.memset(sp[:, 2, :], 0.0))
            for k in range(ATANH_TERMS, 0, -1):
                setup(dve.scalar_tensor_tensor(out=sp[:, 2, :], in0=sp[:, 2, :], scalar=1.0 / (2 * k + 1),
                                               in1=sp[:, 4, :], op0=ALU.add, op1=ALU.mult))
            setup(dve.scalar_tensor_tensor(out=sp[:, 2, :], in0=sp[:, 2, :], scalar=1.0, in1=sp[:, 3, :],
                                           op0=ALU.add, op1=ALU.mult))
            setup(dve.tensor_scalar(sp[:, 4, :], vec[:, :, 7], 0.0, 8.0, ALU.max, ALU.mult))
            setup(dve.scalar_tensor_tensor(out=decay[:], in0=sp[:, 2, :], scalar=16.0, in1=sp[:, 4, :],
                                           op0=ALU.mult, op1=ALU.add))
            setup(dve.tensor_scalar(neg_decay[:], decay[:], -1.0, None, ALU.mult))
            assert steps[0] == SETUP_STEPS

            for c in range(C):
                conv(0, c)
            for i in range(NB + 1):
                if i < NB - 1:
                    if i == 0:
                        dve.wait_ge(s_xrest, 16)
                    layernorm(0, i + 1)
                if i <= 1:
                    normalize(0, i + 1)
                if i == 0:
                    rest_of_t(0, i + 1, x1t_hi, x1t_lo)
                if i < NB:
                    multiplier_squared(i)
                if 1 < i < NB - 1:
                    normalize(0, i + 1)
                if 2 <= i < NB:
                    route_logits(i - 2)
                if i < NB:
                    scan(i)
                if i == NB:
                    route_weights(NB - 4)
                    route_distance(NB - 3)
                    gated_up(0, 0, 0)
                if 0 < i < NB - 1:
                    rest_of_t(0, i + 1, x1t_hi, x1t_lo)
                if i >= 1:
                    softmax_shift(i - 1)
                if 2 <= i < NB - 1:
                    route_distance(i - 2)
                if i < NB - 1:
                    conv(i + 1, 0)
                if i < NB:
                    x1(i)
                    layernorm(1, i)
                if i == 0:
                    normalize(1, i)
                if i == NB:
                    route_logits(NB - 2)
                    route_ranks(NB - 3)
                    gated_up(0, 1, 0)
                    softmax_sum(NB - 1)
                    route_weights(NB - 3)
                if i < NB - 1:
                    conv(i + 1, 1)
                if 0 < i < NB:
                    normalize(1, i)
                if i == NB - 1:
                    route_ranks(NB - 4)
                if i >= 1:
                    rest_of_o(i - 1)
                if 1 <= i < NB:
                    softmax_sum(i - 1)
                if i == NB:
                    gated_up(1, 0, 1)
                if i < NB:
                    rest_of_t(1, i, x2t_hi, x2t_lo)
                if i >= 1:
                    x2(i - 1)
                    layernorm(2, i - 1)
                    normalize(2, i - 1)
            gated_up(1, 1, 1)
            accumulate(0, 0, 0)
            route_distance(NB - 2)
            route_ranks(NB - 2)
            gated_up(2, 0, 0)
            route_weights(NB - 2)
            gated_up(2, 1, 0)
            route_logits(NB - 1)
            accumulate(1, 0, 1)
            gated_ups(3, 1)
            route_distance(NB - 1)
            accumulate(2, 0, 2)
            route_ranks(NB - 1)
            route_weights(NB - 1)
            with dve.Fori(0, E // 2 - 1) as pair:
                for j in range(LOOPED, LOOPED + PAIR):
                    gated_ups(pair * PAIR + j, j % 2)
                    accumulate(pair * PAIR + (j - 1), pair * 2 + (j - 1) // STEPS, (j - 1) % STEPS)
            for n in range((E - 2) * STEPS + LOOPED, E * STEPS + 1):
                if n < E * STEPS:
                    gated_ups(n, n % 2)
                accumulate(n - 1, (n - 1) // STEPS, (n - 1) % STEPS)


def lay_rows(w):
    return w.reshape(2, 128, -1).transpose(1, 0, 2)


def kernel(**inputs):
    import numpy as np
    import concourse.bacc as bacc
    from concourse.bass_utils import run_bass_kernel_spmd

    v = {n: np.asarray(a) for n, a in inputs.items()}
    B, S, d = v["x"].shape
    tokens = B * S

    def block_diagonal(w):
        out = np.zeros((2, 8, 16, 8, 16), w.dtype)
        for n in range(8):
            out[:, n, :, n, :] = w.reshape(2, 8, 16, 16)[:, n]
        return out.reshape(2, 128, 128).transpose(1, 0, 2)

    def flat(*parts):
        return np.ascontiguousarray(np.concatenate([p.reshape(128, -1) for p in parts], axis=1))

    def channels(a):
        return a.reshape(2, 128).T.reshape(128, 2, 1)

    w_stage1 = flat(block_diagonal(v["L0_attn_ig_w"]),
                    block_diagonal(v["L0_attn_ag_w"]), lay_rows(v["L0_attn_W_resid"].T))
    w_qko = flat(*(lay_rows(v[n].T) for n in ("L0_xattn_wq", "L0_xattn_wk", "L0_xattn_wo")))
    w_stage2 = flat(lay_rows(v["L0_xattn_wv"].T), lay_rows(v["L0_ffn_Wr"]))
    vecs = np.ascontiguousarray(np.concatenate(
        [channels(v["L0_attn_conv_w"][i]) for i in range(4)]
        + [channels(v[n]) for n in ("L0_attn_conv_b", "L0_attn_ig_b", "L0_attn_ag_b", "L0_attn_a_param")], axis=2))
    experts = np.stack([v["L0_ffn_Wg"], v["L0_ffn_Wu"], v["L0_ffn_Wd"]], axis=1)
    experts = experts.reshape(experts.shape[0], 3, 2, 128, 256).transpose(0, 3, 1, 2, 4)
    ctx_t = v["ctx_2048"].reshape(tokens // BLK, BLK, 2, 128).transpose(0, 3, 2, 1)
    arrays = {
        "x": np.ascontiguousarray(v["x"].reshape(tokens, d)),
        "ctx": np.ascontiguousarray(v["ctx_2048"].reshape(tokens, d)),
        "ctx_t": np.ascontiguousarray(ctx_t),
        "w_xy": flat(lay_rows(v["L0_attn_W_xy"].T)),
        "w_qko": w_qko,
        "w_stage1": w_stage1,
        "w_stage2": w_stage2,
        "channel_vecs": vecs,
        "w_experts": np.ascontiguousarray(experts).reshape(experts.shape[0], 128, -1),
        "temperature": np.ascontiguousarray(v["L0_ffn_temperature"]),
    }
    nc = bacc.Bacc("TRN2", target_bir_lowering=False, num_devices=1)
    args = [nc.dram_tensor(n, a.shape, mybir.dt.from_np(a.dtype), kind="ExternalInput").ap() for n, a in arrays.items()]
    out = nc.dram_tensor("out", (tokens, d), F32, kind="ExternalOutput").ap()
    decoder_kernel(nc, *args, out)
    result = run_bass_kernel_spmd(nc, [arrays], core_ids=[0])
    return result.results[0]["out"].reshape(B, S, d)
```
